# Optimizing a Trainium2 kernel written in Bass

```python
import numpy as np
import jax
import jax.numpy as jnp

def _softmax(x, axis=-1):
    return jax.nn.softmax(x, axis=axis)

def _gelu(x):
    return jax.nn.gelu(x, approximate=True)

def _silu(x):
    return jax.nn.silu(x)

def _sigmoid(x):
    return jax.nn.sigmoid(x)

def _layernorm(x, axis=-1, eps=1e-05):
    m = jnp.mean(x, axis=axis, keepdims=True)
    v = jnp.var(x, axis=axis, keepdims=True)
    return (x - m) / jnp.sqrt(v + eps)

def _scatter_add(tgt, idx, src, axis=0):
    return tgt.at[idx].add(src)

def _segment_sum(src, seg, n):
    return jax.ops.segment_sum(src, seg, n)
kernel_name = 'mk_vit_tower_cls_d1_tok_img4096_r4_da1356'

def setup_inputs(seed: int=0):
    np.random.seed(seed)
    _w = jnp.asarray

    def _rec_inputs():
        import jax
        import jax.numpy as jnp
        _rk = jax.random.key(seed)
        x = -0.00348982 + 0.707501 * jax.random.normal(jax.random.fold_in(_rk, 1), (64, 128, 64, 2), jnp.float32)
        cls_tok = 0.02 * jax.random.normal(jax.random.fold_in(_rk, 5), (1, 1, 1024), jnp.float32)
        return (x, cls_tok)
    x, cls_tok = _rec_inputs()

    def _L0_tok_setup():
        import jax, jax.numpy as jnp
        import numpy as np
        H, N, S, CH, LEN = (128, 64, 128, 1, 1024)

        def _s4d_kernel(log_dt, C, B, inv_A_real, A_imag, L):
            dt = jnp.exp(log_dt)
            Cc = C[..., 0] + 1j * C[..., 1]
            Bc = B[..., 0] + 1j * B[..., 1]
            A = -jnp.exp(inv_A_real) + 1j * A_imag
            rep = H // A.shape[0]
            A = jnp.tile(A, (rep, 1))
            Bc = jnp.tile(Bc, (rep, 1))
            dtA = A * dt[:, None]
            Cc = Bc[None, :, :] * Cc
            Cc = Cc * (jnp.exp(dtA) - 1.0) / A
            ell = jnp.arange(L, dtype=jnp.float32)
            V = jnp.exp(dtA[:, :, None] * ell)
            K = 2.0 * jnp.einsum('chn,hnl->chl', Cc, V).real
            return K.astype(jnp.float32)
        key = jax.random.key(seed)
        k1, k2 = jax.random.split(key, 2)
        log_dt = jax.random.uniform(k1, (H,), minval=float(np.log(0.001)), maxval=float(np.log(0.1))).astype(jnp.float32)
        inv_A_real = jnp.full((S, N), float(np.log(0.5)), dtype=jnp.float32)
        A_imag = jnp.tile((np.pi * jnp.arange(N, dtype=jnp.float32))[None, :], (S, 1))
        B = jnp.stack([jnp.ones((S, N), jnp.float32), jnp.zeros((S, N), jnp.float32)], axis=-1)
        C = (jax.random.normal(k2, (CH, H, N, 2)) * 0.5 ** 0.5).astype(jnp.float32)
        return {'log_dt': log_dt, 'C': C, 'B': B, 'inv_A_real': inv_A_real, 'A_imag': A_imag, 'L': LEN}
    _L0_tok_all = _L0_tok_setup()
    _L0_tok_in = {k: v for k, v in _L0_tok_all.items() if k in ('log_dt', 'B', 'inv_A_real', 'A_imag')}
    del _L0_tok_all

    def _L0_attn_setup():
        import jax, jax.numpy as jnp
        import numpy as np
        N_STATE = 64
        SEQ_L = 1024
        BATCH, HCH = (16, 128)
        DT_MIN, DT_MAX = (0.001, 0.1)

        def _make_DPLR_HiPPO(N):
            P = np.sqrt(1 + 2 * np.arange(N))
            A = P[:, None] * P[None, :]
            A = np.tril(A) - np.diag(np.arange(N))
            nhippo = -A
            p = 0.5 * np.sqrt(2 * np.arange(1, N + 1) + 1.0)
            q = 2 * p
            S = nhippo + p[:, None] * q[None, :]
            Lambda, V = np.linalg.eig(S)
            Vc = V.conj().T
            p_t = Vc @ p
            q_t = Vc @ q.conj()
            return (Lambda, p_t, q_t, Vc)

        def _ri(z):
            return np.stack([z.real, z.imag], axis=-1).astype(np.float32)

        def _cplx(x_ri):
            return x_ri[..., 0] + 1j * x_ri[..., 1]

        def _s4_kernel(Lambda, p, q, B, Ct, step, L):
            Omega = jnp.exp(-2j * jnp.pi * (jnp.arange(L) / L))
            g = 2.0 / step * ((1.0 - Omega) / (1.0 + Omega))
            c = 2.0 / (1.0 + Omega)
            denom = g[:, None] - Lambda[None, :]
            cauchy = lambda v: (v[None, :] / denom).sum(-1)
            k00 = cauchy(Ct.conj() * B)
            k01 = cauchy(Ct.conj() * p)
            k10 = cauchy(q.conj() * B)
            k11 = cauchy(q.conj() * p)
            at_roots = c * (k00 - k01 * (1.0 / (1.0 + k11)) * k10)
            return jnp.fft.ifft(at_roots, L).real
        key = jax.random.key(seed)
        k_u, k_ct, k_b, k_d, k_ls = jax.random.split(key, 5)
        Lambda, p, q, Vc = _make_DPLR_HiPPO(N_STATE)
        u = jax.random.normal(k_u, (BATCH, HCH, SEQ_L), dtype=jnp.float32)
        Ct_ri = jax.random.normal(k_ct, (1, N_STATE, 2), dtype=jnp.float32) / np.sqrt(N_STATE)
        Bp = jax.random.normal(k_b, (N_STATE, 1), dtype=jnp.float32) / np.sqrt(N_STATE)
        D = jax.random.uniform(k_d, (1,), dtype=jnp.float32)
        log_step = jax.random.uniform(k_ls, (1,), dtype=jnp.float32, minval=np.log(DT_MIN), maxval=np.log(DT_MAX))
        return {'u': u, 'Lambda_ri': jnp.asarray(_ri(Lambda)), 'p_ri': jnp.asarray(_ri(p)), 'q_ri': jnp.asarray(_ri(q)), 'Vc_ri': jnp.asarray(_ri(Vc)), 'Ct_ri': Ct_ri, 'Bp': Bp, 'D': D, 'log_step': log_step}
    _L0_attn_all = _L0_attn_setup()
    _L0_attn_in = {k: v for k, v in _L0_attn_all.items() if k in ('Lambda_ri', 'p_ri', 'q_ri', 'Vc_ri', 'Ct_ri', 'Bp', 'D', 'log_step')}
    del _L0_attn_all

    def _L0_ffn_setup():
        import jax, jax.numpy as jnp
        import numpy as np

        def sparsemax(z):
            E = z.shape[-1]
            z_sorted = -jnp.sort(-z, axis=-1)
            z_cum = jnp.cumsum(z_sorted, axis=-1)
            k = jnp.arange(1, E + 1, dtype=z.dtype)
            support = 1.0 + k * z_sorted > z_cum
            k_z = jnp.sum(support, axis=-1, keepdims=True)
            tau_sum = jnp.take_along_axis(z_cum, k_z.astype(jnp.int32) - 1, axis=-1)
            tau = (tau_sum - 1.0) / k_z.astype(z.dtype)
            return jnp.maximum(z - tau, 0.0)
        key = jax.random.key(seed)
        ks = jax.random.split(key, 6)
        B, S, D_IN, D_OUT, E, R = (8, 512, 1024, 1024, 8, 16)
        x = jax.random.normal(ks[0], (B, S, D_IN), dtype=jnp.float32)
        W_base = jax.random.normal(ks[1], (D_OUT, D_IN), dtype=jnp.float32) * D_IN ** (-0.5)
        b_base = jax.random.normal(ks[2], (D_OUT,), dtype=jnp.float32) * 0.01
        W_router = jax.random.normal(ks[3], (E, D_IN), dtype=jnp.float32) * D_IN ** (-0.5)
        b_router = jnp.zeros((E,), dtype=jnp.float32)
        lora_A = jax.random.normal(ks[4], (E, D_IN, R), dtype=jnp.float32) * D_IN ** (-0.5)
        lora_B = jnp.zeros((E, R, D_OUT), dtype=jnp.float32)
        return {'x': x, 'W_base': W_base, 'b_base': b_base, 'W_router': W_router, 'b_router': b_router, 'lora_A': lora_A, 'lora_B': lora_B}
    _L0_ffn_all = _L0_ffn_setup()
    _L0_ffn_in = {k: v for k, v in _L0_ffn_all.items() if k in ('W_base', 'b_base', 'W_router', 'b_router', 'lora_A', 'lora_B')}
    del _L0_ffn_all
    return {'x': x, 'cls_tok': cls_tok, 'L0_tok_log_dt': _L0_tok_in['log_dt'], 'L0_tok_B': _L0_tok_in['B'], 'L0_tok_inv_A_real': _L0_tok_in['inv_A_real'], 'L0_tok_A_imag': _L0_tok_in['A_imag'], 'L0_attn_Lambda_ri': _L0_attn_in['Lambda_ri'], 'L0_attn_p_ri': _L0_attn_in['p_ri'], 'L0_attn_q_ri': _L0_attn_in['q_ri'], 'L0_attn_Vc_ri': _L0_attn_in['Vc_ri'], 'L0_attn_Ct_ri': _L0_attn_in['Ct_ri'], 'L0_attn_Bp': _L0_attn_in['Bp'], 'L0_attn_D': _L0_attn_in['D'], 'L0_attn_log_step': _L0_attn_in['log_step'], 'L0_ffn_W_base': _L0_ffn_in['W_base'], 'L0_ffn_b_base': _L0_ffn_in['b_base'], 'L0_ffn_W_router': _L0_ffn_in['W_router'], 'L0_ffn_b_router': _L0_ffn_in['b_router'], 'L0_ffn_lora_A': _L0_ffn_in['lora_A'], 'L0_ffn_lora_B': _L0_ffn_in['lora_B']}

def reference(x, cls_tok, L0_tok_log_dt, L0_tok_B, L0_tok_inv_A_real, L0_tok_A_imag, L0_attn_Lambda_ri, L0_attn_p_ri, L0_attn_q_ri, L0_attn_Vc_ri, L0_attn_Ct_ri, L0_attn_Bp, L0_attn_D, L0_attn_log_step, L0_ffn_W_base, L0_ffn_b_base, L0_ffn_W_router, L0_ffn_b_router, L0_ffn_lora_A, L0_ffn_lora_B):
    import jax
    import jax.numpy as jnp

    def _L0_tok_ref(log_dt, C, B, inv_A_real, A_imag, L):
        import jax, jax.numpy as jnp
        import numpy as np
        H, N, S, CH, LEN = (128, 64, 128, 1, 1024)

        def _s4d_kernel(log_dt, C, B, inv_A_real, A_imag, L):
            dt = jnp.exp(log_dt)
            Cc = C[..., 0] + 1j * C[..., 1]
            Bc = B[..., 0] + 1j * B[..., 1]
            A = -jnp.exp(inv_A_real) + 1j * A_imag
            rep = H // A.shape[0]
            A = jnp.tile(A, (rep, 1))
            Bc = jnp.tile(Bc, (rep, 1))
            dtA = A * dt[:, None]
            Cc = Bc[None, :, :] * Cc
            Cc = Cc * (jnp.exp(dtA) - 1.0) / A
            ell = jnp.arange(L, dtype=jnp.float32)
            V = jnp.exp(dtA[:, :, None] * ell)
            K = 2.0 * jnp.einsum('chn,hnl->chl', Cc, V).real
            return K.astype(jnp.float32)
        return _s4d_kernel(log_dt, C, B, inv_A_real, A_imag, L)

    def _L0_attn_ref(u, Lambda_ri, p_ri, q_ri, Vc_ri, Ct_ri, Bp, D, log_step):
        import jax, jax.numpy as jnp
        import numpy as np
        N_STATE = 64
        SEQ_L = 1024
        BATCH, HCH = (16, 128)
        DT_MIN, DT_MAX = (0.001, 0.1)

        def _make_DPLR_HiPPO(N):
            P = np.sqrt(1 + 2 * np.arange(N))
            A = P[:, None] * P[None, :]
            A = np.tril(A) - np.diag(np.arange(N))
            nhippo = -A
            p = 0.5 * np.sqrt(2 * np.arange(1, N + 1) + 1.0)
            q = 2 * p
            S = nhippo + p[:, None] * q[None, :]
            Lambda, V = np.linalg.eig(S)
            Vc = V.conj().T
            p_t = Vc @ p
            q_t = Vc @ q.conj()
            return (Lambda, p_t, q_t, Vc)

        def _ri(z):
            return np.stack([z.real, z.imag], axis=-1).astype(np.float32)

        def _cplx(x_ri):
            return x_ri[..., 0] + 1j * x_ri[..., 1]

        def _s4_kernel(Lambda, p, q, B, Ct, step, L):
            Omega = jnp.exp(-2j * jnp.pi * (jnp.arange(L) / L))
            g = 2.0 / step * ((1.0 - Omega) / (1.0 + Omega))
            c = 2.0 / (1.0 + Omega)
            denom = g[:, None] - Lambda[None, :]
            cauchy = lambda v: (v[None, :] / denom).sum(-1)
            k00 = cauchy(Ct.conj() * B)
            k01 = cauchy(Ct.conj() * p)
            k10 = cauchy(q.conj() * B)
            k11 = cauchy(q.conj() * p)
            at_roots = c * (k00 - k01 * (1.0 / (1.0 + k11)) * k10)
            return jnp.fft.ifft(at_roots, L).real
        L = u.shape[-1]
        Lambda = _cplx(Lambda_ri)
        p = _cplx(p_ri)
        q = _cplx(q_ri)
        Vc = _cplx(Vc_ri)
        Ct = _cplx(Ct_ri).reshape(-1)
        B = (Vc @ Bp.astype(Vc.dtype)).reshape(-1)
        step = jnp.exp(log_step)[0]
        K = _s4_kernel(Lambda, p, q, B, Ct, step, L).astype(u.dtype)
        n = 2 * L
        y = jnp.fft.irfft(jnp.fft.rfft(u, n=n) * jnp.fft.rfft(K, n=n), n=n)[..., :L]
        return y + D[0] * u

    def _L0_ffn_ref(x, W_base, b_base, W_router, b_router, lora_A, lora_B):
        import jax, jax.numpy as jnp
        import numpy as np

        def sparsemax(z):
            E = z.shape[-1]
            z_sorted = -jnp.sort(-z, axis=-1)
            z_cum = jnp.cumsum(z_sorted, axis=-1)
            k = jnp.arange(1, E + 1, dtype=z.dtype)
            support = 1.0 + k * z_sorted > z_cum
            k_z = jnp.sum(support, axis=-1, keepdims=True)
            tau_sum = jnp.take_along_axis(z_cum, k_z.astype(jnp.int32) - 1, axis=-1)
            tau = (tau_sum - 1.0) / k_z.astype(z.dtype)
            return jnp.maximum(z - tau, 0.0)
        base_out = jnp.einsum('bsd,od->bso', x, W_base) + b_base
        logits = jnp.einsum('bsd,ed->bse', x, W_router) + b_router
        weights = sparsemax(logits)
        h = jnp.einsum('bsd,edr->bser', x, lora_A)
        expert_out = jnp.einsum('bser,bse,ero->bso', h, weights, lora_B)
        return base_out + expert_out
    h = _L0_tok_ref(L0_tok_log_dt, x, L0_tok_B, L0_tok_inv_A_real, L0_tok_A_imag, 1024)
    h = jnp.concatenate([jnp.broadcast_to(cls_tok, (h.shape[0], 1, h.shape[2])), h], axis=1)
    h = h + _L0_attn_ref(_layernorm(h, axis=-1), L0_attn_Lambda_ri, L0_attn_p_ri, L0_attn_q_ri, L0_attn_Vc_ri, L0_attn_Ct_ri, L0_attn_Bp, L0_attn_D, L0_attn_log_step)
    h = h + _L0_ffn_ref(_layernorm(h, axis=-1), L0_ffn_W_base, L0_ffn_b_base, L0_ffn_W_router, L0_ffn_b_router, L0_ffn_lora_A, L0_ffn_lora_B)
    return h

_drawn_inputs = setup_inputs


def setup_inputs(seed=0):
    import zlib

    import numpy as np

    out = dict(_drawn_inputs(seed))
    spreads = {'L0_tok_inv_A_real': (-0.6931471824645996, 0.2),
     'L0_ffn_b_router': (0.0, 0.381),
     'L0_ffn_lora_B': (0.0, 0.1)}
    factors = {'L0_attn_Lambda_ri': 3.768, 'L0_attn_Bp': 2.833, 'L0_ffn_b_base': 6.047}
    for name, (base, spread) in spreads.items():
        noise = np.random.default_rng([zlib.crc32(name.encode()), seed]).standard_normal(out[name].shape)
        drawn = base * np.exp(spread * noise) if base else spread * noise
        out[name] = jnp.asarray(drawn.astype(out[name].dtype))
    for name, factor in factors.items():
        out[name] = (out[name] * factor).astype(out[name].dtype)
    return out
```

```python
from contextlib import ExitStack

import numpy as np

import concourse.bass as bass
from concourse import mybir

F32 = mybir.dt.float32
F32R = mybir.dt.float32r
I32 = mybir.dt.int32
ALU = mybir.AluOpType
ACT = mybir.ActivationFunctionType
AX = mybir.AxisListType

P = 128
C = 64
H = 128
N = 64
L = 1024
NB = L // P
E = 8
RK = 16
ER = E * RK
AR = ER + E
TH = P // C
TILES = H // TH
NE, NF = 8, 16
PW = NB + NE + NF
HC = 16
EPS = 1e-5
MAGIC = 12582912.0
MAGIC13 = 1536.0
TWO_PI = float(np.float32(6.2831850))
INV_2PI = 0.15915494309189535
PI_PARTS = (6.28125, 0.0019350051879882812, 3.0198490e-07)
LN2_PARTS = (0.693359375, -2.12194440e-4)


def exp_series():
    out, f = [], 1.0
    for k in range(1, 9):
        f *= k
        out.append(1.0 / f)
    return out[::-1]


def shape_tables():
    f = np.float32
    ident = np.eye(P, dtype=f)
    power = np.concatenate([128 * np.arange(NB), 16 * np.arange(NE), np.arange(NF)])
    phase = np.zeros((P, PW))
    phase[0::2, 0:NB + NE] = 0.25
    powers = np.concatenate([np.broadcast_to(power, (P, PW)), phase], 1).astype(f)
    half = np.pi * np.arange(L) / L
    half = np.stack([np.cos(half), np.sin(half)]).astype(f)
    ps = 2 * np.pi * np.outer(np.arange(P), np.arange(P)) / P
    r, s, q = np.arange(NB), np.arange(P), np.arange(NB)
    ang = 2 * np.pi * q[None, None, :] * (128 * r[None, :, None] + s[:, None, None]) / L
    twiddle = np.concatenate([np.cos(ang), -np.sin(ang)], 2) / L
    k = np.arange(1, E + 1)
    mean_of_top = np.tril(np.ones((E, E))) / k[:, None]
    sparse = np.concatenate([mean_of_top.ravel(), -1.0 / k])
    return {
        "k_ident": np.concatenate([ident, ident[::-1], np.cos(ps), np.sin(ps)], 1).astype(f),
        "k_powers": powers,
        "k_half": half,
        "k_twiddle": twiddle.reshape(P, NB * 2 * NB).astype(f),
        "k_sparse": np.broadcast_to(sparse, (P, E * E + E)).astype(f).copy(),
    }


def raw(t, offset, dims):
    return bass.AP(tensor=t.tensor, offset=offset, ap=[list(d) for d in dims])


def build(nc, a, out, dbg=None):
    with ExitStack() as ctx:
        def sb(name, shape, dt=F32):
            return ctx.enter_context(nc.sbuf_tensor(name, shape, dt))

        def sem(name):
            return ctx.enter_context(nc.semaphore(name))

        def psum(name, n):
            return ctx.enter_context(nc.psum_tensor(name, [P, n], F32))

        ident4 = sb("ident4", [P, 4 * P])
        ident, exch = ident4[:, 0:P], ident4[:, P:2 * P]
        dft_cos, dft_sin = ident4[:, 2 * P:3 * P], ident4[:, 3 * P:4 * P]
        ident_r, ones_r = sb("ident_r", [P, P], F32R), sb("ones_r", [P, P], F32R)
        ones = sb("ones", [P, P])
        w_hi, w_lo = sb("w_hi", [P, NB, L], F32R), sb("w_lo", [P, NB, L], F32R)
        ar_hi, ar_lo = sb("ar_hi", [P, NB, AR], F32R), sb("ar_lo", [P, NB, AR], F32R)
        lb_hi, lb_lo = sb("lb_hi", [P, L], F32R), sb("lb_lo", [P, L], F32R)
        t_hi, t_lo = sb("t_hi", [P, L], F32R), sb("t_lo", [P, L], F32R)
        neg_cum = sb("neg_cum", [P, L])
        bias = sb("bias", [P, L])
        b_router = sb("b_router", [P, E])
        sparse = sb("sparse", [P, E * E + E])
        table = sb("table", [P, H, 2, PW])
        U, W = table[:, :, 0, 0:NB], table[:, :, 1, 0:NB]
        z16_a, z16_b = table[:, :, 0, NB:NB + NE], table[:, :, 1, NB:NB + NE]
        z1_sin, z1_cos = table[:, :, 0, NB + NE:PW], table[:, :, 1, NB + NE:PW]
        x_in = sb("x_in", [C, 2, TH, P])
        cls_row = sb("cls_row", [1, L])
        x_swap = sb("x_swap", [C, 2, TH, P])
        g_a, g_b = sb("g_a", [P, TH, NB, C]), sb("g_b", [P, TH, NB, C])
        q_a, q_b = sb("q_a", [P, TH, P]), sb("q_b", [P, TH, P])
        h1_hi, h1_lo = sb("h1_hi", [P, NB, P], F32R), sb("h1_lo", [P, NB, P], F32R)
        h1, h2 = sb("h1", [P, L]), sb("h2", [P, L])
        h2_hi = sb("h2_hi", [P, 2, NB, P], F32R)
        h2_lo = sb("h2_lo", [P, 2, NB, P], F32R)
        h2_bias = sb("h2_bias", [P, 2, L])
        res = sb("res", [P, 2, L])
        st = sb("st", [P, 2, 2, 6])
        mv1, mv2 = sb("mv1", [P, 2]), sb("mv2", [P, 2])
        rstd1, rstd2 = sb("rstd1", [P, 1]), sb("rstd2", [P, 2, 1])
        minus_half, eps = sb("minus_half", [P, 1]), sb("eps", [P, 1])
        v_eps = sb("v_eps", [P, 2])
        logit, top, tau, gate = (sb(n, [P, E]) for n in ("logit", "top", "tau", "gate"))
        top_sums = sb("top_sums", [P, E, E])
        tau1 = sb("tau1", [P, 1])
        hw = sb("hw", [P, ER])
        hw_hi, hw_lo = sb("hw_hi", [P, P], F32R), sb("hw_lo", [P, P], F32R)
        planes_t = sb("planes_t", [P, 7, P])
        w_mean = sb("w_mean", [P, NB])
        zero_row = sb("zero_row", [1, P])
        kpad = nc.dram_tensor("kpad", [1, P + L], F32, kind="Internal").ap()

        p_x = psum("p_x", 512)
        p_a = psum("p_a", 1024)
        p_b = psum("p_b", 1024)
        p_o = psum("p_o", 1024)
        p_s = psum("p_s", 512)

        names = ("ld_const ld_ssm ld_s4 ld_w0 ld_w1 ld_ar ld_misc ld_x0 ld_x1 k_out k_back stored0 stored1 ld_end "
                 "v_chain a_chain g_chain p_chain consts_g "
                 "s4_v s4_sum s4_at s4_b s4_k s4_kt s4_ktc t_rev t_hi_s t_split cum_mm cum_done "
                 "planes planes_t planes_c tab_le tab_f tab_e tab_sc tab_done "
                 "ssm_r ssm_s s4_d s4_sq lb_hi_s ar_cent v_step g_step pl tab_w table_done vm w_mean w_cent w_tr w_hi_s w_lo_s r_tr r_evac ar_mean ar_done lb_done "
                 "x_sw x_t g_prod g_done q_done h1T h1hi h1lo h1row h1_sb mvar1 rs1 y_mm h2_s h2T h2hi h2lo "
                 "mvar2 rs2 h2b ar_mm gated hwT hw_split o_mm fin").split()
        S = {n: sem(n) for n in names}
        block = ctx.enter_context(nc.Block())

        LD_S4 = 16 * (1 + 8 + 2 + 7)

        def chain(eng, name):
            count = [0]

            def link(ins):
                count[0] += 1
                ins.then_inc(S[name], 1)
                eng.wait_ge(S[name], count[0])
            return link

        table_flat = table[:, :, :, :].rearrange("p h a b -> p (h a b)")
        scratch = table_flat[:, L:3 * L + P]
        small = table_flat[:, 4 * L:4 * L + 32 * (N + 2)].rearrange("p (n w) -> p n w", n=32)

        def sm(n, w=N):
            return small[:, n, 0:w]

        s4_cos, s4_sin = (g[:, :, :, :].rearrange("p t a c -> p (t a c)") for g in (g_a, g_b))
        ssm_b = q_a[:, 1, :].rearrange("p (n r) -> p n r", r=2)
        vc = q_b[:, 1, :].rearrange("p (n r) -> p n r", r=2)
        twiddle = q_a[:, 0, :]
        powers = q_b[:, 0, 0:2 * PW]

        ar_raw = scratch[:, 0:NB * AR].rearrange("p (k n) -> p k n", k=NB)
        planes = scratch[:, NB * AR + 64:NB * AR + 64 + 7 * P].rearrange("p (f n) -> p f n", f=7)
        t_rev = scratch[:, 0:L]
        lora_b = neg_cum[:, :]
        router_rows = table[0:E, :, :, :].rearrange("e h a b -> e (h a b)")[:, 0:L]
        k_rows = hw[0:NB, :]
        x_rows = a["x"].rearrange("c h n r -> c h (n r)")

        def flat(t):
            return t[:, :, :, :].rearrange("p h a c -> p (h a c)")

        def piece(t, k):
            return t[:, k * HC * PW:(k + 1) * HC * PW].rearrange("p (h j) -> p h j", h=HC)

        tab_e, tab_l = piece(flat(g_a), 0), piece(flat(g_a), 1)
        tab_f, tab_k = piece(flat(g_b), 0), piece(flat(g_b), 1)
        tab_fa, tab_fb = piece(h2, 0), piece(h2, 1)
        tab_x, tab_sa = piece(h1, 0), piece(h1, 1)
        tab_sb = piece(res[:, 0, :], 0)
        by_head_psum = p_a[:, :].rearrange("p (h a c) -> p h a c", h=TH, a=NB)

        def by_head(t):
            return t[:, :, :].rearrange("p a (h c) -> p h a c", h=TH)

        def bcast(ap, axis, count):
            shape = list(ap.shape)
            shape.insert(axis, count)
            return ap.unsqueeze(axis).broadcast_to(shape)

        def steps(eng, step):
            for t in range(3):
                step(t, t % 2, (t - 1) // 2)
            with eng.Fori(1, TILES // 2 - 1) as i:
                step(2 * i + 1, 1, i)
                step(2 * i + 2, 0, i)
            for t in range(TILES - 1, TILES + 2):
                step(t, t % 2, (t - 1) // 2)

        def step_chain(eng, name):
            count = [0]

            def own(ins):
                count[0] += 1
                ins.then_inc(S[name], 1)

            def start():
                count[0] = 0
                eng.sem_clear(S[name])
            own.start, own.wait = start, lambda: eng.wait_ge(S[name], count[0])
            return own

        @block.sync
        def _(sp):
            def load(dst, src, s):
                sp.dma_start(dst, src).then_inc(S[s], 16)

            load(small[:, 0, 0:N], a["L0_tok_inv_A_real"], "ld_ssm")
            load(small[:, 0, N:N + 1], a["L0_tok_log_dt"].rearrange("(h a) -> h a", a=1), "ld_ssm")
            load(small[:, 0, N + 1:N + 2], raw(a["L0_attn_log_step"], 0, [[0, P], [1, 1]]), "ld_ssm")
            load(small[:, 1, 0:N], a["L0_tok_A_imag"], "ld_ssm")
            load(ssm_b, a["L0_tok_B"], "ld_ssm")
            load(ident4[:, :], a["k_ident"], "ld_const")
            for i in range(2):
                load(res[:, i, :], a["L0_ffn_W_base"][i * P:(i + 1) * P, :], f"ld_w{i % 2}")
            load(powers, a["k_powers"], "ld_s4")
            for n, name in enumerate(("L0_attn_Lambda_ri", "L0_attn_Ct_ri", "L0_attn_p_ri", "L0_attn_q_ri")):
                for half in range(2):
                    load(small[half * N:half * N + N, 4, 2 * n:2 * n + 2], raw(a[name], 0, [[2, N], [1, 2]]), "ld_s4")
            for half in range(2):
                load(vc[half * N:half * N + N], a["L0_attn_Vc_ri"], "ld_s4")
            load(sm(7), raw(a["L0_attn_Bp"], 0, [[0, P], [1, N]]), "ld_s4")
            load(s4_cos, raw(a["k_half"], 0, [[0, P], [1, L]]), "ld_s4")
            load(s4_sin, raw(a["k_half"], L, [[0, P], [1, L]]), "ld_s4")
            load(sm(8, NB), raw(a["k_half"], 0, [[NB, P], [1, NB]]), "ld_s4")
            load(sm(9, NB), raw(a["k_half"], L, [[NB, P], [1, NB]]), "ld_s4")
            load(small[0:1, 10, 0:1], raw(a["L0_attn_D"], 0, [[1, 1], [1, 1]]), "ld_s4")
            load(twiddle, a["k_twiddle"], "ld_s4")
            for k in range(NB):
                load(ar_raw[:, k, 0:ER].rearrange("p (e r) -> p e r", e=E),
                     raw(a["L0_ffn_lora_A"], k * P * RK, [[RK, P], [L * RK, E], [1, RK]]), "ld_ar")
            load(router_rows, a["L0_ffn_W_router"], "ld_ar")
            load(lora_b, a["L0_ffn_lora_B"].rearrange("e r o -> (e r) o"), "ld_misc")
            load(bias[:, :], raw(a["L0_ffn_b_base"], 0, [[0, P], [1, L]]), "ld_misc")
            load(b_router[:, :], raw(a["L0_ffn_b_router"], 0, [[0, P], [1, E]]), "ld_misc")
            load(sparse[:, :], a["k_sparse"], "ld_misc")
            load(cls_row[:, :], a["cls_tok"].rearrange("a b l -> (a b) l"), "ld_misc")
            for t in (1, 2):
                load(x_in[:, t % 2, :, :], x_rows[:, TH * (t - 1):TH * t, :], f"ld_x{t % 2}")
            for i in range(2, NB):
                sp.wait_ge(S["w_cent"], i - 1)
                load(res[:, i % 2, :], a["L0_ffn_W_base"][i * P:(i + 1) * P, :], f"ld_w{i % 2}")
            sp.wait_ge(S["s4_ktc"], 1)
            sp.dma_start(raw(kpad, P, [[P, NB], [1, P]]), k_rows).then_inc(S["k_out"], 16)
            sp.dma_start(raw(kpad, 0, [[P, 1], [1, P]]), zero_row[:, :]).then_inc(S["k_out"], 16)
            sp.wait_ge(S["k_out"], 32)
            sp.wait_ge(S["ar_done"], 2)
            sp.dma_start(t_rev, raw(kpad, 1, [[1, P], [1, L]])).then_inc(S["k_back"], 16)

            def load_x(t, par):
                load(x_in[:, par, :, :], x_rows[:, bass.ds(TH * (t - 1), TH), :], f"ld_x{par}")

            def store(t, par):
                for k in range(TH):
                    dst = out[:, bass.ds(TH * t + k - 1, 1), :].rearrange("c a l -> c (a l)")
                    sp.dma_start(dst, res[k * C:(k + 1) * C, par, :]).then_inc(S[f"stored{par}"], 16)

            sp.wait_ge(S["x_t"], 1)
            load_x(3, 1)
            sp.wait_ge(S["fin"], 2)
            sp.dma_start(out[:, 0:1, :].rearrange("c a l -> c (a l)"), res[0:C, 0, :]).then_inc(S["stored0"], 16)

            def turn(t, par, more):
                if more:
                    sp.wait_ge(S["x_t"], t + 1)
                    load_x(t + 3, 1 - par)
                sp.wait_ge(S["fin"], 2 * t + 2)
                store(t, par)
            with sp.Fori(0, TILES // 2 - 2) as i:
                turn(2 * i + 1, 1, True)
                turn(2 * i + 2, 0, True)
            for t in range(TILES - 3, TILES + 1):
                turn(t, t % 2, t + 3 <= TILES)
            sp.wait_ge(S["stored0"], 16 + 32 * (TILES // 2))
            sp.wait_ge(S["stored1"], 32 * (TILES // 2))

        def toeplitz(pe, lhs_hi, lhs_lo, out_bank, name):
            for bank in range(2):
                lo, hi = 512 * bank, 512 * bank + 512
                blocks = range(hi // P)
                for j in blocks:
                    first = max(lo, j * P)
                    o = out_bank[:, first:hi]
                    w = slice(first - j * P, hi - j * P)
                    pe.matmul(o, lhs_hi(j), t_hi[:, w], start=(j == 0), stop=False)
                    last = pe.matmul(o, lhs_hi(j), t_lo[:, w], start=False, stop=(j == blocks[-1] and lhs_lo is None))
                    if lhs_lo is not None:
                        last = pe.matmul(o, lhs_lo(j), t_hi[:, w], start=False, stop=(j == blocks[-1]))
                last.then_inc(S[name], 1)

        @block.tensor
        def _(pe):
            def turn_w(i):
                pe.wait_ge(S["w_cent"], i + 1)
                if i >= 2:
                    pe.wait_ge(S["w_hi_s"], i - 1)
                    pe.wait_ge(S["w_lo_s"], i - 1)
                bank = (p_a, p_b)[i % 2]
                for k in range(NB):
                    last = pe.transpose(bank[:, k * P:(k + 1) * P], h2_bias[:, i % 2, k * P:(k + 1) * P], ident)
                last.then_inc(S["w_tr"], 1)

            pe.wait_ge(S["ld_const"], 16)
            turn_w(0)
            turn_w(1)
            pe.wait_ge(S["planes"], 1)
            for f in range(7):
                last = pe.transpose(p_o[:, f * P:(f + 1) * P], planes[:, f, :], ident)
            last.then_inc(S["planes_t"], 1)
            pe.wait_ge(S["s4_v"], 1)
            for q in range(NB):
                last = pe.matmul(p_s[:, NB * q:NB * q + NB], h1[:, q::NB], small[:, 31, 0:8], start=True, stop=True)
            last.then_inc(S["s4_sum"], 1)
            pe.wait_ge(S["s4_at"], 1)
            pe.matmul(p_s[:, 64:80], dft_cos, small[:, 29, 0:16], start=True, stop=False)
            pe.matmul(p_s[:, 64:80], dft_sin, small[:, 30, 0:16], start=False, stop=True).then_inc(S["s4_b"], 1)
            pe.wait_ge(S["s4_k"], 1)
            pe.transpose(p_s[0:NB, 128:256], small[:, 28, 0:NB], ident).then_inc(S["s4_kt"], 1)
            for i in range(2, NB):
                turn_w(i)
            pe.wait_ge(S["ld_ar"], 16 * (NB + 1))
            for k in range(NB):
                last = pe.transpose(p_x[:, E * k:E * k + E], router_rows[:, k * P:(k + 1) * P], ident[0:E, 0:E])
            last.then_inc(S["r_tr"], 1)
            pe.wait_ge(S["r_evac"], 1)
            for k in range(NB):
                last = pe.matmul(p_x[:, 128:128 + AR], ones[:, :], ar_raw[:, k, :], start=(k == 0), stop=(k == NB - 1))
            last.then_inc(S["ar_mean"], 1)
            pe.wait_ge(S["k_back"], 16)
            pe.wait_ge(S["planes_c"], 1)
            for bank in range(2):
                last = pe.matmul(p_o[:, 512 * bank:512 * bank + 512], exch, t_rev[:, 512 * bank:512 * bank + 512],
                                 start=True, stop=True)
            last.then_inc(S["t_rev"], 1)
            pe.wait_ge(S["t_hi_s"], 1)
            pe.wait_ge(S["t_split"], 1)
            pe.wait_ge(S["consts_g"], 2)
            toeplitz(pe, lambda j: ones_r[:, :], None, p_o, "cum_mm")
            pe.wait_ge(S["cum_done"], 1)
            pe.wait_ge(S["ar_cent"], 1)
            pe.wait_ge(S["ar_done"], 2)
            pe.wait_ge(S["ld_misc"], 80)
            pe.wait_ge(S["w_hi_s"], NB)
            pe.wait_ge(S["w_lo_s"], NB)
            pa = p_a[:, :].rearrange("p (h a c) -> p h a c", h=TH, a=NB)
            for h in range(TH):
                for k in range(NB):
                    last = pe.matmul(pa[:, h, k, :], cls_row[:, k * P:(k + 1) * P], ones[0:1, 0:C], start=True, stop=True)
            last.then_inc(S["h1T"], 1)

            def three(o, x_hi, x_lo, y_hi, y_lo, start, stop):
                pe.matmul(o, x_hi, y_hi, start=start, stop=False)
                pe.matmul(o, x_hi, y_lo, start=False, stop=False)
                return pe.matmul(o, x_lo, y_hi, start=False, stop=stop)

            def step(t, par, turn):
                n = t if isinstance(t, int) else None
                cur, feed, nxt = n is None or n <= TILES, n is None or n >= 1, n is None or n < TILES
                prv = 1 - par
                if nxt:
                    pe.wait_ge(S["x_sw"], t + 1)
                    if feed:
                        pe.wait_ge(S["g_prod"], t)
                if cur:
                    pe.wait_ge(S["h1hi"], t + 1)
                    pe.wait_ge(S["h1lo"], t + 1)
                    if feed:
                        pe.wait_ge(S["h2lo"], t)
                    for k in range(NB):
                        o = p_b[:, k * P:(k + 1) * P]
                        pe.matmul(o, h1_hi[:, k, :], ident_r[:, :], start=True, stop=False)
                        last = pe.matmul(o, h1_lo[:, k, :], ident_r[:, :], start=False, stop=True)
                    last.then_inc(S["h1row"], 1)
                if nxt:
                    for h in range(TH):
                        pe.transpose(p_x[:, h * C:(h + 1) * C], x_in[:, prv, h, :], ident[0:C, 0:C])
                        last = pe.transpose(p_x[:, (TH + h) * C:(TH + h + 1) * C], x_swap[:, prv, h, :], ident[0:C, 0:C])
                    last.then_inc(S["x_t"], 1)
                if cur:
                    toeplitz(pe, lambda j: h1_hi[:, j, :], lambda j: h1_lo[:, j, :], p_a, "y_mm")
                if feed:
                    pe.wait_ge(S["gated"], t)
                    pe.transpose(p_s[:, 256:384], hw[:, :], ident).then_inc(S["hwT"], 1)
                    feed_forward(t, prv, 0, n)
                if cur:
                    pe.wait_ge(S["h2_s"], 2 * t + 2)
                    pe.wait_ge(S["h1_sb"], t + 1)
                    for k in range(NB):
                        last = pe.transpose(p_b[:, k * P:(k + 1) * P], h2[:, k * P:(k + 1) * P], ident)
                    last.then_inc(S["h2T"], 1)
                if nxt:
                    pe.wait_ge(S["g_done"], t + 1)
                    pe.wait_ge(S["q_done"], t + 1)
                    for h in range(TH):
                        last = pe.matmul(p_a[:, h * 512:(h + 1) * 512], q_a[:, h, :],
                                         g_a[:, h, :, :].rearrange("p a c -> p (a c)"), start=True, stop=True)
                    last.then_inc(S["h1T"], 1)
                if feed:
                    feed_forward(t, prv, 1, n)
                if cur:
                    pe.wait_ge(S["h2hi"], t + 1)
                    pe.wait_ge(S["h2lo"], t + 1)
                    for k in range(NB):
                        last = three(p_s[:, 0:AR], h2_hi[:, par, k, :], h2_lo[:, par, k, :], ar_hi[:, k, :], ar_lo[:, k, :],
                                     k == 0, k == NB - 1)
                    last.then_inc(S["ar_mm"], 1)

            def feed_forward(t, prv, half, n):
                cols = slice(512 * half, 512 * half + 512)
                if n is None or n >= 2:
                    pe.wait_ge(S["fin"], 2 * t - 3 + half)
                for k in range(NB):
                    three(p_o[:, cols], h2_hi[:, prv, k, :], h2_lo[:, prv, k, :], w_hi[:, k, cols], w_lo[:, k, cols], k == 0, False)
                if half == 0:
                    pe.wait_ge(S["hw_split"], 2 * t)
                three(p_o[:, cols], hw_hi[:, :], hw_lo[:, :], lb_hi[:, cols], lb_lo[:, cols], False, True).then_inc(S["o_mm"], 1)

            steps(pe, step)

        @block.scalar
        def _(act):
            link = chain(act, "a_chain")

            def mean_w(i):
                act.wait_ge(S[f"ld_w{i % 2}"], 16 * (i // 2 + 1))
                if i >= 2:
                    act.wait_ge(S["w_tr"], i - 1)
                act.activation(h2_bias[:, i % 2, :], res[:, i % 2, :], ACT.Copy, scale=-1.0 / L,
                               accum_out=w_mean[:, i:i + 1]).then_inc(S["w_mean"], 1)

            def turned(bank):
                return bank[:, :].rearrange("p (k o) -> p k o", k=NB)

            def high_w(i):
                act.wait_ge(S["w_tr"], i + 1)
                act.activation(w_hi[:, :, i * P:(i + 1) * P], turned((p_a, p_b)[i % 2]), ACT.Copy).then_inc(S["w_hi_s"], 1)

            mean_w(0)
            mean_w(1)
            act.wait_ge(S["ld_const"], 16)
            act.activation(ident_r[:, :], ident, ACT.Copy).then_inc(S["consts_g"], 1)
            act.wait_ge(S["p_chain"], 1)
            act.activation(ones_r[:, :], ones[:, :], ACT.Copy).then_inc(S["consts_g"], 1)
            high_w(0)
            high_w(1)
            act.wait_ge(S["ssm_r"], 1)
            act.activation(sm(27), sm(26), ACT.Sin).then_inc(S["ssm_s"], 1)
            act.activation(sm(25), sm(26), ACT.Sin, scale=0.5).then_inc(S["ssm_s"], 1)
            act.wait_ge(S["s4_d"], 1)
            act.activation(s4_sin, h1[:, :], ACT.Square).then_inc(S["s4_sq"], 1)
            act.activation(s4_cos, h2[:, :], ACT.Square).then_inc(S["s4_sq"], 1)
            for i in range(2, NB):
                mean_w(i)
                high_w(i)
            act.wait_ge(S["ld_misc"], 80)
            act.activation(lb_hi[:, :], lora_b, ACT.Copy).then_inc(S["lb_hi_s"], 1)
            act.wait_ge(S["ar_cent"], 1)
            act.activation(ar_hi[:, :, :], ar_raw, ACT.Copy).then_inc(S["ar_done"], 1)
            act.wait_ge(S["t_rev"], 1)
            act.activation(t_hi[:, :], p_o[:, :], ACT.Copy).then_inc(S["t_hi_s"], 1)
            act.wait_ge(S["cum_mm"], 2)
            act.wait_ge(S["lb_done"], 1)
            act.activation(neg_cum[:, :], p_o[:, :], ACT.Copy, scale=-1.0).then_inc(S["cum_done"], 1)
            for ch in range(H // HC):
                act.wait_ge(S["tab_f"], ch + 1)
                act.activation(tab_sa, tab_fa, ACT.Sin, scale=TWO_PI).then_inc(S["tab_sc"], 1)
                act.activation(tab_sb, tab_fb, ACT.Sin, scale=TWO_PI).then_inc(S["tab_sc"], 1)
                act.wait_ge(S["tab_le"], 2 * ch + 2)
                act.activation(tab_x, tab_e, ACT.Exp).then_inc(S["tab_sc"], 1)

            def step(t, par, turn):
                n = t if isinstance(t, int) else None
                cur, feed, nxt = n is None or n <= TILES, n is None or n >= 1, n is None or n < TILES
                if cur:
                    act.wait_ge(S["h1row"], t + 1)
                    if feed:
                        act.wait_ge(S["h2_s"], 2 * t)
                    act.activation(h1[:, :], p_b[:, :], ACT.Copy).then_inc(S["h1_sb"], 1)
                if feed:
                    act.wait_ge(S["hwT"], t)
                    if n is None or n >= 2:
                        act.wait_ge(S["o_mm"], 2 * t - 2)
                    act.activation(hw_hi[:, :], p_s[:, 256:384], ACT.Copy).then_inc(S["hw_split"], 1)
                if cur:
                    act.wait_ge(S["h2T"], t + 1)
                    act.activation(h2_hi[:, par, :, :].rearrange("p k c -> p (k c)"), p_b[:, :], ACT.Copy).then_inc(S["h2hi"], 1)
                if nxt:
                    act.wait_ge(S["h1T"], t + 2)
                    act.activation(by_head(h1_hi), by_head_psum, ACT.Copy).then_inc(S["h1hi"], 1)

            act.wait_ge(S["h1T"], 1)
            act.activation(by_head(h1_hi), by_head_psum, ACT.Copy).then_inc(S["h1hi"], 1)
            steps(act, step)

        @block.gpsimd
        def _(pool):
            link = chain(pool, "g_chain")
            pool.memset(ones[:, :], 1.0).then_inc(S["p_chain"], 1)
            pool.memset(zero_row[:, :], 0.0).then_inc(S["p_chain"], 1)
            pool.memset(minus_half[:, :], -0.5).then_inc(S["p_chain"], 1)
            pool.memset(eps[:, :], EPS).then_inc(S["p_chain"], 1)
            for i in range(NB):
                pool.wait_ge(S["w_mean"], i + 1)
                pool.tensor_scalar(h2_bias[:, i % 2, :], res[:, i % 2, :], w_mean[:, i:i + 1], None, ALU.add)\
                    .then_inc(S["w_cent"], 1)
            pool.wait_ge(S["planes_c"], 1)
            pool.wait_ge(S["ld_s4"], LD_S4)
            pool.wait_ge(S["s4_v"], 1)
            for ch in range(H // HC):
                hs = slice(ch * HC, (ch + 1) * HC)
                if ch:
                    pool.wait_ge(S["tab_done"], ch)
                for f, o in ((0, tab_e), (2, tab_l)):
                    pool.tensor_tensor(o, bcast(planes_t[:, f, hs], 2, PW), bcast(powers[:, 0:PW], 1, HC), ALU.mult)\
                        .then_inc(S["tab_le"], 1)

            def swap(par):
                for r in range(2):
                    ins = pool.tensor_copy(x_swap[:, par, :, r::2], x_in[:, par, :, 1 - r::2])
                ins.then_inc(S["x_sw"], 1)

            own = step_chain(pool, "g_step")

            def make_q(t):
                hs = bass.ds(TH * (t - 1), TH)
                q4 = [q[:, :, :].rearrange("p h (i j) -> p h i j", i=NE) for q in (q_a, q_b)]
                return hs, q4

            def step(t, par, turn):
                n = t if isinstance(t, int) else None
                cur, feed, nxt = n is None or n <= TILES, n is None or n >= 1, n is None or n < TILES
                own.start()
                if cur:
                    pool.wait_ge(S["mvar1"], t + 1)
                    if feed:
                        pool.wait_ge(S["h2_s"], 2 * t)
                    own(pool.tensor_tensor(v_eps[:, 0:1], mv1[:, 1:2], eps[:, :], ALU.add))
                    own.wait()
                    pool.tensor_tensor(rstd1[:, :], v_eps[:, 0:1], minus_half[:, :], ALU.pow).then_inc(S["rs1"], 1)
                if nxt:
                    hs, (qa, qb) = make_q(t + 1)
                    pool.wait_ge(S["h1T"], t + 1)
                    own(pool.tensor_tensor(qa, bcast(z16_a[:, hs, :], 3, NF), bcast(z1_cos[:, hs, :], 2, NE), ALU.mult))
                    own(pool.tensor_tensor(qb, bcast(z16_b[:, hs, :], 3, NF), bcast(z1_sin[:, hs, :], 2, NE), ALU.mult))
                    own.wait()
                    pool.tensor_tensor(q_a[:, :, :], q_a[:, :, :], q_b[:, :, :], ALU.add).then_inc(S["q_done"], 1)
                    pool.wait_ge(S["g_prod"], t + 1)
                    pool.tensor_tensor(flat(g_a), flat(g_a), flat(g_b), ALU.add).then_inc(S["g_done"], 1)
                if cur:
                    pool.wait_ge(S["h2_s"], 2 * t + 2)
                    if n is None or n >= 2:
                        pool.wait_ge(S["fin"], 2 * t - 2)
                    pool.tensor_tensor(h2_bias[:, par, :], h2[:, :], bias[:, :], ALU.add).then_inc(S["h2b"], 1)
                    pool.wait_ge(S["mvar2"], t + 1)
                    own(pool.tensor_tensor(v_eps[:, 1:2], mv2[:, 1:2], eps[:, :], ALU.add))
                    own.wait()
                    if n is None or n < TILES - 1:
                        if n is None or n >= 1:
                            pool.wait_ge(S["x_t"], t)
                        pool.wait_ge(S[f"ld_x{par}"], 16 * (turn + 2))
                    pool.tensor_tensor(rstd2[:, par, :], v_eps[:, 1:2], minus_half[:, :], ALU.pow).then_inc(S["rs2"], 1)
                if n is None or n < TILES - 1:
                    swap(par)

            pool.wait_ge(S["ld_x1"], 16)
            swap(1)
            pool.wait_ge(S["table_done"], 1)
            steps(pool, step)

        @block.vector
        def _(dve):
            link = chain(dve, "v_chain")

            def ts(o, i, s1, s2=None, op0=ALU.mult, op1=None):
                link(dve.tensor_scalar(o, i, s1, s2, op0, op1) if op1 is not None else dve.tensor_scalar(o, i, s1, None, op0))

            def tt(o, x, y, op):
                link(dve.tensor_tensor(o, x, y, op))

            def stt(o, x, s, y, op0=ALU.mult, op1=ALU.add):
                link(dve.scalar_tensor_tensor(out=o, in0=x, scalar=s, in1=y, op0=op0, op1=op1))

            def copy(o, i):
                link(dve.tensor_copy(o, i))

            mul, add, sub = ALU.mult, ALU.add, ALU.subtract

            def exp_parts(x, w, k, r, p, two):
                ts(k, x, 1.4426950408889634, MAGIC, mul, add)
                ts(k, k, -MAGIC, -126.0, add, ALU.max)
                stt(r, k, -LN2_PARTS[0], x)
                stt(r, k, -LN2_PARTS[1], r)
                series = exp_series()
                ts(p, r, series[0])
                for c in series[1:]:
                    stt(p, p, c, r, add, mul)
                ts(k, k, 127.0, 127.0, ALU.min, add)
                ts(two.bitcast(I32), k, float(2 ** 23))

            dve.wait_ge(S["ld_ssm"], 80)
            w = N + 2
            x0, k, r, p, two, ex = (sm(n, w) for n in (0, 13, 14, 15, 16, 17))
            exp_parts(x0, w, k, r, p, two)
            stt(ex, p, 1.0, two, add, mul)
            ea, dt, stp = ex[:, 0:N], ex[:, N:N + 1], ex[:, N + 1:N + 2]
            a_im, alpha, om = sm(1), sm(18), sm(19)
            ts(alpha, ea, dt, -1.0, mul, mul)
            ts(om, a_im, dt)
            k, r, p, two, em1 = (sm(n) for n in (13, 14, 15, 16, 20))
            exp_parts(alpha, N, k, r, p, two)
            tt(p, two, p, mul)
            stt(em1, two, -1.0, p, add, add)
            ts(k, om, INV_2PI, MAGIC, mul, add)
            ts(k, k, -MAGIC, None, add)
            phase = sm(26)
            stt(phase, k, -PI_PARTS[0], om)
            stt(phase, k, -PI_PARTS[1], phase)
            stt(phase, k, -PI_PARTS[2], phase)
            dve.tensor_scalar(phase, phase, 3.1415925, -3.1415925, ALU.min, ALU.max).then_inc(S["ssm_r"], 1)
            dve.wait_ge(S["ssm_r"], 1)
            turns, turns_h, turns_l = sm(21), sm(22), sm(23)
            ts(turns, phase, INV_2PI)
            ts(turns_h, turns, MAGIC13, -MAGIC13, add, add)
            tt(turns_l, turns, turns_h, sub)
            dve.wait_ge(S["ssm_s"], 2)
            s1, s2 = sm(27), sm(25)
            er, ei = sm(13), sm(14)
            tt(s2, s2, s2, mul)
            ts(er, s2, -2.0, 1.0, mul, add)
            tt(er, er, em1, mul)
            stt(er, s2, -2.0, er)
            stt(ei, em1, 1.0, s1, add, mul)
            den, tmp, nr, ni = sm(15), sm(16), sm(18 + 6), sm(12)
            tt(den, a_im, a_im, mul)
            tt(tmp, ea, ea, mul)
            tt(den, den, tmp, add)
            link(dve.reciprocal(den, den))
            tt(nr, ei, a_im, mul)
            tt(tmp, er, ea, mul)
            tt(nr, nr, tmp, sub)
            tt(ni, er, a_im, mul)
            tt(tmp, ei, ea, mul)
            tt(ni, ni, tmp, add)
            stt(nr, nr, 2.0, den, mul, mul)
            stt(ni, ni, 2.0, den, mul, mul)
            cr, ci = sm(13), sm(14)
            br, bi = ssm_b[:, :, 0], ssm_b[:, :, 1]
            tt(cr, nr, br, mul)
            tt(tmp, ni, bi, mul)
            tt(cr, cr, tmp, add)
            tt(ci, nr, bi, mul)
            tt(tmp, ni, br, mul)
            tt(ci, ci, tmp, sub)
            pv = planes.rearrange("p f (n r) -> p f n r", r=2)
            for f, t in ((0, alpha), (1, turns_h), (2, turns_l)):
                dve.tensor_copy(pv[:, f], bcast(t, 2, 2)).then_inc(S["pl"], 1)
            for f, even, odd in ((3, (cr, 1.0), (ci, 1.0)), (4, (ci, 1.0), (cr, -1.0)),
                                 (5, (ci, -1.0), (cr, -1.0)), (6, (cr, 1.0), (ci, -1.0))):
                for half, (t, sign) in enumerate((even, odd)):
                    dve.tensor_scalar(pv[:, f, :, half], t, sign, None, mul).then_inc(S["pl"], 1)
            dve.wait_ge(S["pl"], 11)
            copy(tmp, cr)
            dve.sem_inc(S["planes"], 1)

            dve.wait_ge(S["ld_s4"], LD_S4)
            lam = small[:, 4, 0:2]
            sv = small[:, 16, 0:4].rearrange("p (v r) -> p v r", v=2)
            prod = small[:, 17:19, 0:N]
            tt(prod, vc.rearrange("p n r -> p r n"), bcast(sm(7), 1, 2), mul)
            link(dve.tensor_reduce(sv[:, 0, :], prod, AX.X, add))
            copy(sv[:, 1, :], small[:, 4, 4:6])
            vv = small[:, 17, 0:8].rearrange("p (m v r) -> p m v r", m=2, v=2)
            t2 = small[:, 18, 0:2]
            for m, at in enumerate((2, 6)):
                mr, mi = small[:, 4, at:at + 1], small[:, 4, at + 1:at + 2]
                ts(t2, sv[:, :, 0], mr)
                stt(vv[:, m, :, 0], sv[:, :, 1], mi, t2)
                ts(t2, sv[:, :, 0], mi)
                stt(vv[:, m, :, 1], sv[:, :, 1], mr, t2, mul, sub)
            vm = small[:, 31, 0:8].rearrange("p (j r) -> p j r", r=2)
            vj = small[:, 17, 0:8].rearrange("p (j r) -> p j r", r=2)
            copy(vm[0:N], vj[0:N])
            ts(vm[N:P, :, 0], vj[N:P, :, 1], -1.0)
            copy(vm[N:P, :, 1], vj[N:P, :, 0])
            g2, nl = small[:, 19, 0:1], small[:, 19, 2:4]
            link(dve.reciprocal(g2, stp))
            ts(g2, g2, 2.0)
            ts(nl, lam, -1.0)
            ts(h1[:, :], s4_cos, nl[:, 0:1])
            ts(h2[:, :], s4_sin, g2)
            dve.scalar_tensor_tensor(out=h2[:, :], in0=s4_cos, scalar=nl[:, 1:2], in1=h2[:, :], op0=mul, op1=add)\
                .then_inc(S["s4_d"], 1)
            dve.wait_ge(S["s4_sq"], 2)
            tt(s4_sin, s4_sin, s4_cos, add)
            link(dve.reciprocal(s4_cos, s4_sin))
            tt(h1[0:N, :], h1[0:N, :], s4_cos[0:N, :], mul)
            stt(h1[N:P, :], h2[N:P, :], -1.0, s4_cos[N:P, :], mul, mul)
            dve.sem_inc(S["s4_v"], 1)

            dve.wait_ge(S["planes_t"], 1)
            dve.tensor_copy(planes_t[:, :, :].rearrange("p f h -> p (f h)"), p_o[:, 0:7 * P]).then_inc(S["planes_c"], 1)

            def low_w(i):
                dve.wait_ge(S["w_hi_s"], i + 1)
                cols = slice(i * P, (i + 1) * P)
                dve.tensor_tensor(w_lo[:, :, cols], (p_a, p_b)[i % 2][:, :].rearrange("p (k o) -> p k o", k=NB),
                                  w_hi[:, :, cols].bitcast(F32), sub).then_inc(S["w_lo_s"], 1)

            low_w(0)
            low_w(1)

            dve.wait_ge(S["s4_sum"], 1)
            sums = small[:, 16, 0:N]
            copy(sums, p_s[:, 0:N])
            s = sums.rearrange("p (q j) -> p j q", q=NB)
            c8, s8 = sm(8, NB), sm(9, NB)
            tr, ti, den, tmp, xr, xi, yr, yi = (sm(n, NB) for n in (17, 18, 19, 20, 21, 22, 23, 24))
            tt(tr, c8, s[:, 6], mul)
            ts(tr, tr, 1.0, None, add)
            tt(ti, c8, s[:, 7], mul)
            tt(den, tr, tr, mul)
            tt(tmp, ti, ti, mul)
            tt(den, den, tmp, add)
            link(dve.reciprocal(den, den))
            tt(xr, s[:, 2], s[:, 4], mul)
            tt(tmp, s[:, 3], s[:, 5], mul)
            tt(xr, xr, tmp, sub)
            tt(xr, xr, c8, mul)
            tt(xi, s[:, 2], s[:, 5], mul)
            tt(tmp, s[:, 3], s[:, 4], mul)
            tt(xi, xi, tmp, add)
            tt(xi, xi, c8, mul)
            tt(yr, xr, tr, mul)
            tt(tmp, xi, ti, mul)
            tt(yr, yr, tmp, add)
            tt(yr, yr, den, mul)
            tt(yi, xi, tr, mul)
            tt(tmp, xr, ti, mul)
            tt(yi, yi, tmp, sub)
            tt(yi, yi, den, mul)
            tt(yr, s[:, 0], yr, sub)
            tt(yi, s[:, 1], yi, sub)
            at1, at2 = small[:, 29, 0:2 * NB], small[:, 30, 0:2 * NB]
            tt(xr, c8, yr, mul)
            tt(tmp, s8, yi, mul)
            tt(at1[:, 0:NB], xr, tmp, sub)
            tt(xr, c8, yi, mul)
            tt(tmp, s8, yr, mul)
            tt(at1[:, NB:], xr, tmp, add)
            ts(at2[:, 0:NB], at1[:, NB:], -1.0)
            copy(at2[:, NB:], at1[:, 0:NB])
            dve.sem_inc(S["s4_at"], 1)
            dve.wait_ge(S["s4_b"], 1)
            kp = small[:, 18:20, 0:N].rearrange("p a b -> p a b")
            spec = sm(17, 2 * NB)
            copy(spec, p_s[:, 64:80])
            tw = twiddle.rearrange("p (r q) -> p r q", r=NB)
            tt(tw, tw, bcast(spec, 1, NB), mul)
            kern = sm(28, NB)
            link(dve.tensor_reduce(kern, tw, AX.X, add))
            tt(kern[0:1, 0:1], kern[0:1, 0:1], small[0:1, 10, 0:1], add)
            dve.sem_inc(S["s4_k"], 1)
            dve.wait_ge(S["s4_kt"], 1)
            dve.tensor_copy(k_rows, p_s[0:NB, 128:256]).then_inc(S["s4_ktc"], 1)
            for i in range(2, NB):
                low_w(i)

            dve.wait_ge(S["r_tr"], 1)
            dve.tensor_copy(ar_raw[:, :, ER:AR], p_x[:, 0:NB * E].rearrange("p (k e) -> p k e", k=NB)).then_inc(S["r_evac"], 1)
            dve.wait_ge(S["ar_mean"], 1)
            dve.scalar_tensor_tensor(out=ar_raw, in0=bcast(p_x[:, 128:128 + AR], 1, NB), scalar=-1.0 / L, in1=ar_raw,
                                     op0=mul, op1=add).then_inc(S["ar_cent"], 1)
            dve.wait_ge(S["ar_done"], 1)
            dve.tensor_tensor(ar_lo[:, :, :], ar_raw, ar_hi[:, :, :].bitcast(F32), sub).then_inc(S["ar_done"], 1)
            dve.wait_ge(S["lb_hi_s"], 1)
            dve.tensor_tensor(lb_lo[:, :], lora_b, lb_hi[:, :].bitcast(F32), sub).then_inc(S["lb_done"], 1)
            dve.wait_ge(S["t_hi_s"], 1)
            dve.tensor_tensor(t_lo[:, :], p_o[:, :], t_hi[:, :].bitcast(F32), sub).then_inc(S["t_split"], 1)

            for ch in range(H // HC):
                hs = slice(ch * HC, (ch + 1) * HC)
                rows = bcast(powers[:, 0:PW], 1, HC)
                tt(tab_f, bcast(planes_t[:, 1, hs], 2, PW), rows, mul)
                tt(tab_f, tab_f, bcast(powers[:, PW:2 * PW], 1, HC), add)
                dve.wait_ge(S["tab_le"], 2 * ch + 2)
                tt(tab_k, tab_f, tab_l, add)
                ts(tab_k, tab_k, MAGIC, -MAGIC, add, add)
                tt(tab_f, tab_f, tab_k, sub)
                tt(tab_fa, tab_f, tab_l, add)
                ts(tab_k, tab_fa, 0.25, None, ALU.is_gt)
                dve.scalar_tensor_tensor(out=tab_fb, in0=tab_fa, scalar=0.25, in1=tab_k, op0=add, op1=sub)\
                    .then_inc(S["tab_f"], 1)
                dve.wait_ge(S["tab_sc"], 3 * ch + 3)
                dve.tensor_tensor(table[:, hs, 0, :], tab_sa, tab_x, mul).then_inc(S["tab_w"], 1)
                dve.tensor_tensor(table[:, hs, 1, :], tab_sb, tab_x, mul).then_inc(S["tab_done"], 1)
                dve.wait_ge(S["tab_done"], ch + 1)
            u8 = [h2[:, :].rearrange("p (h a) -> p h a", h=H), flat(g_a).rearrange("p (h a) -> p h a", h=H),
                  flat(g_b).rearrange("p (h a) -> p h a", h=H)]
            tt(u8[0], U, bcast(planes_t[:, 3, :], 2, NB), mul)
            tt(u8[1], W, bcast(planes_t[:, 4, :], 2, NB), mul)
            tt(u8[0], u8[0], u8[1], add)
            tt(u8[1], U, bcast(planes_t[:, 5, :], 2, NB), mul)
            tt(u8[2], W, bcast(planes_t[:, 6, :], 2, NB), mul)
            tt(W, u8[1], u8[2], add)
            copy(U, u8[0])
            dve.sem_inc(S["table_done"], 1)

            own = step_chain(dve, "v_step")

            def stats(src, s):
                for half in range(2):
                    ins = dve.bn_stats(st[:, s, half, :], src[:, 512 * half:512 * half + 512])
                own(ins)

            def aggregate(s, mv, name):
                own.wait()
                dve.bn_aggr(mv[:, :], st[:, s, :, :].rearrange("p a b -> p (a b)")).then_inc(S[name], 1)

            def products(t):
                dve.wait_ge(S["x_t"], t)
                hs = bass.ds(TH * (t - 1), TH)
                for g, at, pw in ((g_a, 0, U), (g_b, TH * C, W)):
                    x = p_x[:, at:at + TH * C].rearrange("p (h c) -> p h c", h=TH)
                    ins = dve.tensor_tensor(g[:, :, :, :], bcast(x, 2, NB), bcast(pw[:, hs, :], 3, C), mul)
                ins.then_inc(S["g_prod"], 1)

            def gate_step(prv):
                def glink(ins):
                    own(ins)
                    own.wait()
                glink(dve.scalar_tensor_tensor(out=logit[:, :], in0=p_s[:, ER:AR], scalar=rstd2[:, prv, :], in1=b_router[:, :],
                                               op0=mul, op1=add))
                glink(dve.max(top[:, :], logit[:, :]))
                glink(dve.tensor_tensor(top_sums[:, :, :], sparse[:, 0:E * E].rearrange("p (k i) -> p k i", k=E),
                                        bcast(top[:, :], 1, E), mul))
                glink(dve.tensor_reduce(tau[:, :], top_sums[:, :, :], AX.X, add))
                glink(dve.tensor_tensor(tau[:, :], tau[:, :], sparse[:, E * E:E * E + E], add))
                glink(dve.tensor_reduce(tau1[:, :], tau[:, :], AX.X, ALU.max))
                glink(dve.tensor_scalar(gate[:, :], logit[:, :], tau1[:, :], 0.0, sub, ALU.max))
                dve.tensor_tensor(hw[:, :].rearrange("p (e r) -> p e r", e=E), p_s[:, 0:ER].rearrange("p (e r) -> p e r", e=E),
                                  bcast(gate[:, :], 2, RK), mul).then_inc(S["gated"], 1)

            def finish(prv, half):
                cols = slice(512 * half, 512 * half + 512)
                dve.scalar_tensor_tensor(out=res[:, prv, cols], in0=p_o[:, cols], scalar=rstd2[:, prv, :],
                                         in1=h2_bias[:, prv, cols], op0=mul, op1=add).then_inc(S["fin"], 1)

            def step(t, par, turn):
                n = t if isinstance(t, int) else None
                cur, feed, nxt = n is None or n <= TILES, n is None or n >= 1, n is None or n < TILES
                prv = 1 - par
                own.start()
                if cur:
                    dve.wait_ge(S["h1_sb"], t + 1)
                    stats(h1, 0)
                    aggregate(0, mv1, "mvar1")
                if feed:
                    dve.wait_ge(S["ar_mm"], t)
                    dve.wait_ge(S["rs2"], t)
                    gate_step(prv)
                if nxt:
                    if feed:
                        dve.wait_ge(S["h1T"], t + 1)
                    products(t + 1)
                if feed:
                    dve.wait_ge(S["hw_split"], 2 * t - 1)
                    dve.tensor_tensor(hw_lo[:, :], p_s[:, 256:384], hw_hi[:, :].bitcast(F32), sub).then_inc(S["hw_split"], 1)
                if cur:
                    dve.wait_ge(S["rs1"], t + 1)
                    if feed:
                        dve.wait_ge(S["h2T"], t)
                        dve.wait_ge(S["h2b"], t)
                    for half in range(2):
                        cols = slice(512 * half, 512 * half + 512)
                        dve.wait_ge(S["y_mm"], 2 * t + 1 + half)
                        own(dve.scalar_tensor_tensor(out=h2[:, cols], in0=neg_cum[:, cols], scalar=mv1[:, 0:1], in1=p_a[:, cols],
                                                     op0=mul, op1=add))
                    for half in range(2):
                        cols = slice(512 * half, 512 * half + 512)
                        if half == 0:
                            own.wait()
                        dve.scalar_tensor_tensor(out=h2[:, cols], in0=h2[:, cols], scalar=rstd1[:, :], in1=h1[:, cols],
                                                 op0=mul, op1=add).then_inc(S["h2_s"], 1)
                    dve.wait_ge(S["h2_s"], 2 * t + 2)
                    stats(h2, 1)
                    aggregate(1, mv2, "mvar2")
                if feed:
                    dve.wait_ge(S["o_mm"], 2 * t - 1)
                    if n is None or n >= 3:
                        dve.wait_ge(S[f"stored{prv}"], 32 * turn - 16 * par)
                    finish(prv, 0)
                if cur:
                    dve.wait_ge(S["h2hi"], t + 1)
                    dve.tensor_tensor(h2_lo[:, par, :, :].rearrange("p k c -> p (k c)"), p_b[:, :],
                                      h2_hi[:, par, :, :].rearrange("p k c -> p (k c)").bitcast(F32), sub).then_inc(S["h2lo"], 1)
                if nxt:
                    dve.wait_ge(S["h1hi"], t + 2)
                    dve.tensor_tensor(by_head(h1_lo), by_head_psum, by_head(h1_hi).bitcast(F32), sub).then_inc(S["h1lo"], 1)
                if feed:
                    dve.wait_ge(S["o_mm"], 2 * t)
                    finish(prv, 1)

            dve.wait_ge(S["h1hi"], 1)
            dve.tensor_tensor(by_head(h1_lo), by_head_psum, by_head(h1_hi).bitcast(F32), sub).then_inc(S["h1lo"], 1)
            steps(dve, step)


_INS = ["x", "cls_tok", "L0_tok_log_dt", "L0_tok_B", "L0_tok_inv_A_real", "L0_tok_A_imag", "L0_attn_Lambda_ri",
        "L0_attn_p_ri", "L0_attn_q_ri", "L0_attn_Vc_ri", "L0_attn_Ct_ri", "L0_attn_Bp", "L0_attn_D",
        "L0_attn_log_step", "L0_ffn_W_base", "L0_ffn_b_base", "L0_ffn_W_router", "L0_ffn_b_router",
        "L0_ffn_lora_A", "L0_ffn_lora_B"]


def kernel(**inputs):
    import concourse.bacc as _bacc
    from concourse.bass_utils import run_bass_kernel_spmd as _run

    nc = _bacc.Bacc("TRN2", target_bir_lowering=False, num_devices=1)
    arrays = {name: np.ascontiguousarray(inputs[name]) for name in _INS}
    arrays.update(shape_tables())
    aps = {name: nc.dram_tensor(f"in_{name}", x.shape, mybir.dt.from_np(x.dtype), kind="ExternalInput").ap()
           for name, x in arrays.items()}
    out = nc.dram_tensor("out_0", (C, H + 1, L), F32, kind="ExternalOutput").ap()
    build(nc, aps, out)
    r = _run(nc, [{f"in_{name}": x for name, x in arrays.items()}], core_ids=[0])
    return r.results[0]["out_0"]
```

```python
from contextlib import ExitStack

import numpy as np

import concourse.bass as bass
from concourse import mybir

F32 = mybir.dt.float32
F32R = mybir.dt.float32r
I32 = mybir.dt.int32
ALU = mybir.AluOpType
ACT = mybir.ActivationFunctionType
AX = mybir.AxisListType

P = 128
C = 64
H = 128
N = 64
L = 1024
NB = L // P
E = 8
RK = 16
ER = E * RK
AR = ER + E
WA = AR + L
CUTS = (0, 386, 774, WA)
NC = len(CUTS) - 1
TH = P // C
TILES = H // TH
NE, NF = 8, 16
PW = NB + NE + NF
EPS = 1e-5
MAGIC = 12582912.0
MAGIC13 = 1536.0
TWO_PI = float(np.float32(6.2831850))
INV_2PI = 0.15915494309189535
PI_PARTS = (6.28125, 0.0019350051879882812, 3.0198490e-07)
LN2_PARTS = (0.693359375, -2.12194440e-4)


def exp_series():
    out, f = [], 1.0
    for k in range(1, 9):
        f *= k
        out.append(1.0 / f)
    return out[::-1]


def shape_tables():
    f = np.float32
    ident = np.eye(P, dtype=f)
    power = np.concatenate([128 * np.arange(NB), 16 * np.arange(NE), np.arange(NF)])
    phase = np.zeros((P, PW))
    phase[0::2, 0:NB + NE] = 0.25
    powers = np.concatenate([np.broadcast_to(power, (P, PW)), phase], 1).astype(f)
    half = np.pi * np.arange(L) / L
    half = np.stack([np.cos(half), np.sin(half)]).astype(f)
    ps = 2 * np.pi * np.outer(np.arange(P), np.arange(P)) / P
    r, s, q = np.arange(NB), np.arange(P), np.arange(NB)
    ang = 2 * np.pi * q[None, None, :] * (128 * r[None, :, None] + s[:, None, None]) / L
    twiddle = np.concatenate([np.cos(ang), -np.sin(ang)], 2) / L
    k = np.arange(1, E + 1)
    mean_of_top = np.tril(np.ones((E, E))) / k[:, None]
    sparse = np.concatenate([mean_of_top.ravel(), -1.0 / k])
    return {
        "k_ident": np.concatenate([ident, ident[::-1], np.cos(ps), np.sin(ps)], 1).astype(f),
        "k_powers": powers,
        "k_half": half,
        "k_twiddle": twiddle.reshape(P, NB * 2 * NB).astype(f),
        "k_sparse": np.broadcast_to(sparse, (P, E * E + E)).astype(f).copy(),
    }


def raw(t, offset, dims):
    return bass.AP(tensor=t.tensor, offset=offset, ap=[list(d) for d in dims])


def build(nc, a, out, dbg=None):
    with ExitStack() as ctx:
        def sb(name, shape, dt=F32):
            return ctx.enter_context(nc.sbuf_tensor(name, shape, dt))

        def sem(name):
            return ctx.enter_context(nc.semaphore(name))

        def psum(name, n):
            return ctx.enter_context(nc.psum_tensor(name, [P, n], F32))

        ident4 = sb("ident4", [P, 4 * P])
        ident, exch = ident4[:, 0:P], ident4[:, P:2 * P]
        dft_cos, dft_sin = ident4[:, 2 * P:3 * P], ident4[:, 3 * P:4 * P]
        ident_r, ones_r = sb("ident_r", [P, P], F32R), sb("ones_r", [P, P], F32R)
        ones = sb("ones", [P, P])
        wa_hi, wa_lo = sb("wa_hi", [P, NB, WA], F32R), sb("wa_lo", [P, NB, WA], F32R)
        lb_hi, lb_lo = sb("lb_hi", [P, L], F32R), sb("lb_lo", [P, L], F32R)
        t_hi, t_lo = sb("t_hi", [P, L], F32R), sb("t_lo", [P, L], F32R)
        neg_cum = sb("neg_cum", [P, L])
        bias = sb("bias", [P, L])
        b_router = sb("b_router", [P, E])
        sparse = sb("sparse", [P, E * E + E])
        planes_t = sb("planes_t", [P, 7, P])
        size = sb("size", [P, H, PW])
        powers = sb("powers", [P, 2 * PW])
        x_in = sb("x_in", [C, 2, TH, P])
        x_swap = sb("x_swap", [C, 2, TH, P])
        turn_f, turn_l, turn_k = (sb(n, [P, TH, PW]) for n in ("turn_f", "turn_l", "turn_k"))
        angle, wave = sb("angle", [P, 2, TH, PW]), sb("wave", [P, 2, TH, PW])
        power = sb("power", [P, 2, 2, TH, PW])
        uw_prod, uw = sb("uw_prod", [P, 2, 2, TH, NB]), sb("uw", [P, 2, 2, TH, NB])
        g_a, g_b = sb("g_a", [P, TH, NB, C]), sb("g_b", [P, TH, NB, C])
        g_hi, g_lo = sb("g_hi", [P, TH, NB, C], F32R), sb("g_lo", [P, TH, NB, C], F32R)
        q_a, q_b = sb("q_a", [P, TH, P]), sb("q_b", [P, TH, P])
        q_hi, q_lo = sb("q_hi", [P, TH, P], F32R), sb("q_lo", [P, TH, P], F32R)
        h1_t = sb("h1_t", [P, NB, P])
        h1_hi, h1_lo = sb("h1_hi", [P, NB, P], F32R), sb("h1_lo", [P, NB, P], F32R)
        h1, h2 = sb("h1", [P, L]), sb("h2", [P, L])
        h2_hi = sb("h2_hi", [P, 2, NB, P], F32R)
        h2_lo = sb("h2_lo", [P, 2, NB, P], F32R)
        h2_bias = sb("h2_bias", [P, 2, L])
        res = sb("res", [P, 2, L])
        st = sb("st", [P, 2, 2, 6])
        mv1, mv2 = sb("mv1", [P, 2]), sb("mv2", [P, 2])
        rstd1, rstd2 = sb("rstd1", [P, 1]), sb("rstd2", [P, 2, 1])
        minus_half, eps = sb("minus_half", [P, 1]), sb("eps", [P, 1])
        v_eps = sb("v_eps", [P, 2])
        logit, top, tau, gate = (sb(n, [P, E]) for n in ("logit", "top", "tau", "gate"))
        top_sums = sb("top_sums", [P, E, E])
        tau1 = sb("tau1", [P, 1])
        hw = sb("hw", [P, ER])
        hw_hi, hw_lo = sb("hw_hi", [P, P], F32R), sb("hw_lo", [P, P], F32R)
        w_mean = sb("w_mean", [P, NB])
        zero_row = sb("zero_row", [1, P])
        ar_raw_t = sb("ar_raw", [P, NB, AR])
        ar_raw = ar_raw_t[:, :, :]
        kpad = nc.dram_tensor("kpad", [1, P + L], F32, kind="Internal").ap()

        p_x = psum("p_x", 512)
        p_a = psum("p_a", 1024)
        p_b = psum("p_b", 1024)
        p_f = psum("p_f", NC * 512)

        names = ("ld_exp ld_const ld_ssm ld_s4 ld_s4b ld_w0 ld_w1 ld_ar ld_misc ld_x0 ld_x1 k_out k_back stored0 stored1 "
                 "v_chain g_chain p_chain v_step g_step consts_g "
                 "s4_d s4_sq s4_v s4_sum s4_at s4_b s4_k s4_kt s4_ktc t_rev t_hi_s t_split cum_mm cum_done "
                 "ssm_r ssm_s pl planes planes_t planes_c size_e size_done lb_hi_s lb_done "
                 "w_mean w_cent w_tr w_hi_s w_lo_s r_tr r_evac ar_mean ar_cent ar_done "
                 "angles waves turn_low power_done x_sw x_t g_prod g_done g_hi_s g_split q_done q_hi_s q_split "
                 "h1T h1_t h1hi h1lo h1row h1_sb mvar1 rs1 y_mm h2_s h2T h2hi h2lo mvar2 rs2 h2b "
                 "ar_mm base0 gated hwT hw_split o_mm fin").split()
        S = {n: sem(n) for n in names}
        block = ctx.enter_context(nc.Block())

        def chain(eng, name):
            count = [0]

            def link(ins):
                count[0] += 1
                ins.then_inc(S[name], 1)
                eng.wait_ge(S[name], count[0])
            return link

        size_flat = size[:, :, :].rearrange("p h j -> p (h j)")
        small = size_flat[:, 0:32 * (N + 2)].rearrange("p (n w) -> p n w", n=32)
        planes = size_flat[:, 32 * (N + 2):32 * (N + 2) + 7 * P].rearrange("p (f n) -> p f n", f=7)

        def sm(n, w=N):
            return small[:, n, 0:w]

        s4_cos, s4_sin = (g[:, :, :, :].rearrange("p t a c -> p (t a c)") for g in (g_a, g_b))
        ssm_b = q_a[:, 1, :].rearrange("p (n r) -> p n r", r=2)
        vc = q_b[:, 1, :].rearrange("p (n r) -> p n r", r=2)
        twiddle = q_a[:, 0, :]

        t_rev = h1_t[:, :, :].rearrange("p k c -> p (k c)")
        lora_b = neg_cum[:, :]
        cls_row = h2[0:1, :]
        router_rows = h1_t[0:E, :, :].rearrange("p k c -> p (k c)")
        k_rows = hw[0:NB, :]
        x_rows = a["x"].rearrange("c h n r -> c h (n r)")

        def heads(t):
            return bass.ds(TH * (t - 1), TH)

        def flat(t):
            return t[:, :, :, :].rearrange("p h a c -> p (h a c)")

        by_head_psum = p_a[:, :].rearrange("p (h a c) -> p h a c", h=TH, a=NB)

        def by_head(t):
            return t[:, :, :].rearrange("p a (h c) -> p h a c", h=TH)

        def bcast(ap, axis, count):
            shape = list(ap.shape)
            shape.insert(axis, count)
            return ap.unsqueeze(axis).broadcast_to(shape)

        def steps(eng, step):
            for t in range(3):
                step(t, t % 2, (t - 1) // 2)
            with eng.Fori(1, TILES // 2 - 1) as i:
                step(2 * i + 1, 1, i)
                step(2 * i + 2, 0, i)
            for t in range(TILES - 1, TILES + 2):
                step(t, t % 2, (t - 1) // 2)

        def step_chain(eng, name):
            count = [0]

            def own(ins):
                count[0] += 1
                ins.then_inc(S[name], 1)

            def start():
                count[0] = 0
                eng.sem_clear(S[name])
            own.start, own.wait = start, lambda: eng.wait_ge(S[name], count[0])
            return own

        @block.sync
        def _(sp):
            def load(dst, src, s):
                sp.dma_start(dst, src).then_inc(S[s], 16)

            def twice(t):
                return t.rearrange("(a n) r -> a n r", a=2)

            load(small[:, 0, 0:N], a["L0_tok_inv_A_real"], "ld_exp")
            load(small[:, 0, N:N + 1], a["L0_tok_log_dt"].rearrange("(h a) -> h a", a=1), "ld_exp")
            load(small[:, 0, N + 1:N + 2], raw(a["L0_attn_log_step"], 0, [[0, P], [1, 1]]), "ld_exp")
            for n, name in enumerate(("L0_attn_Lambda_ri", "L0_attn_Ct_ri", "L0_attn_p_ri", "L0_attn_q_ri")):
                for half in range(2):
                    load(small[half * N:half * N + N, 4, 2 * n:2 * n + 2], raw(a[name], 0, [[2, N], [1, 2]]), "ld_s4")
            for half in range(2):
                load(vc[half * N:half * N + N], a["L0_attn_Vc_ri"], "ld_s4")
            load(sm(7), raw(a["L0_attn_Bp"], 0, [[0, P], [1, N]]), "ld_s4")
            load(s4_cos, raw(a["k_half"], 0, [[0, P], [1, L]]), "ld_s4")
            load(s4_sin, raw(a["k_half"], L, [[0, P], [1, L]]), "ld_s4")
            for i in range(2):
                load(res[:, i, :], a["L0_ffn_W_base"][i * P:(i + 1) * P, :], f"ld_w{i % 2}")
            load(sm(8, NB), raw(a["k_half"], 0, [[NB, P], [1, NB]]), "ld_s4b")
            load(sm(9, NB), raw(a["k_half"], L, [[NB, P], [1, NB]]), "ld_s4b")
            load(small[0:1, 10, 0:1], raw(a["L0_attn_D"], 0, [[1, 1], [1, 1]]), "ld_s4b")
            load(twiddle, a["k_twiddle"], "ld_s4b")
            load(ident4[:, :], a["k_ident"], "ld_const")
            load(sm(1), a["L0_tok_A_imag"], "ld_ssm")
            load(ssm_b, a["L0_tok_B"], "ld_ssm")
            load(powers[:, :], a["k_powers"], "ld_ssm")
            for i in range(2, 4):
                sp.wait_ge(S["w_cent"], i - 1)
                load(res[:, i % 2, :], a["L0_ffn_W_base"][i * P:(i + 1) * P, :], f"ld_w{i % 2}")
            for k in range(NB):
                load(ar_raw[:, k, 0:ER].rearrange("p (e r) -> p e r", e=E),
                     raw(a["L0_ffn_lora_A"], k * P * RK, [[RK, P], [L * RK, E], [1, RK]]), "ld_ar")
            load(router_rows, a["L0_ffn_W_router"], "ld_ar")
            for i in range(4, NB):
                sp.wait_ge(S["w_cent"], i - 1)
                load(res[:, i % 2, :], a["L0_ffn_W_base"][i * P:(i + 1) * P, :], f"ld_w{i % 2}")
            load(lora_b, a["L0_ffn_lora_B"].rearrange("e r o -> (e r) o"), "ld_misc")
            sp.wait_ge(S["s4_v"], 1)
            load(cls_row, a["cls_tok"].rearrange("a b l -> (a b) l"), "ld_misc")
            for t in (1, 2):
                load(x_in[:, t % 2, :, :], x_rows[:, TH * (t - 1):TH * t, :], f"ld_x{t % 2}")
            load(bias[:, :], raw(a["L0_ffn_b_base"], 0, [[0, P], [1, L]]), "ld_misc")
            load(b_router[:, :], raw(a["L0_ffn_b_router"], 0, [[0, P], [1, E]]), "ld_misc")
            load(sparse[:, :], a["k_sparse"], "ld_misc")
            sp.wait_ge(S["s4_ktc"], 1)
            sp.dma_start(raw(kpad, P, [[P, NB], [1, P]]), k_rows).then_inc(S["k_out"], 16)
            sp.dma_start(raw(kpad, 0, [[P, 1], [1, P]]), zero_row[:, :]).then_inc(S["k_out"], 16)
            sp.wait_ge(S["k_out"], 32)
            sp.wait_ge(S["r_tr"], 1)
            sp.dma_start(t_rev, raw(kpad, 1, [[1, P], [1, L]])).then_inc(S["k_back"], 16)

            def load_x(t, par):
                load(x_in[:, par, :, :], x_rows[:, bass.ds(TH * (t - 1), TH), :], f"ld_x{par}")

            def store(t, par):
                for k in range(TH):
                    dst = out[:, bass.ds(TH * t + k - 1, 1), :].rearrange("c a l -> c (a l)")
                    sp.dma_start(dst, res[k * C:(k + 1) * C, par, :]).then_inc(S[f"stored{par}"], 16)

            sp.wait_ge(S["x_t"], 1)
            load_x(3, 1)
            sp.wait_ge(S["fin"], NC)
            sp.dma_start(out[:, 0:1, :].rearrange("c a l -> c (a l)"), res[0:C, 0, :]).then_inc(S["stored0"], 16)

            def turn(t, par, more):
                if more:
                    sp.wait_ge(S["x_t"], t + 1)
                    load_x(t + 3, 1 - par)
                sp.wait_ge(S["fin"], NC * t + NC)
                store(t, par)
            with sp.Fori(0, TILES // 2 - 2) as i:
                turn(2 * i + 1, 1, True)
                turn(2 * i + 2, 0, True)
            for t in range(TILES - 3, TILES + 1):
                turn(t, t % 2, t + 3 <= TILES)
            sp.wait_ge(S["stored0"], 16 + 32 * (TILES // 2))
            sp.wait_ge(S["stored1"], 32 * (TILES // 2))

        def toeplitz(pe, lhs_hi, lhs_lo, out_bank, name):
            for bank in range(2):
                lo, hi = 512 * bank, 512 * bank + 512
                blocks = range(hi // P)
                for j in blocks:
                    first = max(lo, j * P)
                    o = out_bank[:, first:hi]
                    w = slice(first - j * P, hi - j * P)
                    pe.matmul(o, lhs_hi(j), t_hi[:, w], start=(j == 0), stop=False)
                    last = pe.matmul(o, lhs_hi(j), t_lo[:, w], start=False, stop=(j == blocks[-1] and lhs_lo is None))
                    if lhs_lo is not None:
                        last = pe.matmul(o, lhs_lo(j), t_hi[:, w], start=False, stop=(j == blocks[-1]))
                last.then_inc(S[name], 1)

        def product(c):
            return slice(512 * c, 512 * c + CUTS[c + 1] - CUTS[c]), slice(CUTS[c], CUTS[c + 1])

        p_s = p_f[:, 1024:1536]
        w_turned = (p_b[:, :], p_f[:, 0:1024])

        @block.tensor
        def _(pe):
            def turn_w(i):
                pe.wait_ge(S["w_cent"], i + 1)
                if i >= 2:
                    pe.wait_ge(S["w_hi_s"], i - 1)
                    pe.wait_ge(S["w_lo_s"], i - 1)
                for k in range(NB):
                    last = pe.transpose(w_turned[i % 2][:, k * P:(k + 1) * P], h2_bias[:, i % 2, k * P:(k + 1) * P], ident)
                last.then_inc(S["w_tr"], 1)

            pe.wait_ge(S["s4_v"], 1)
            for q in range(NB):
                last = pe.matmul(p_s[:, NB * q:NB * q + NB], h1[:, q::NB], small[:, 31, 0:8], start=True, stop=True)
            last.then_inc(S["s4_sum"], 1)
            pe.wait_ge(S["ld_const"], 16)
            turn_w(0)
            turn_w(1)
            pe.wait_ge(S["s4_at"], 1)
            pe.matmul(p_s[:, 64:80], dft_cos, small[:, 29, 0:16], start=True, stop=False)
            pe.matmul(p_s[:, 64:80], dft_sin, small[:, 30, 0:16], start=False, stop=True).then_inc(S["s4_b"], 1)
            pe.wait_ge(S["s4_k"], 1)
            pe.transpose(p_s[0:NB, 128:256], small[:, 28, 0:NB], ident).then_inc(S["s4_kt"], 1)
            turn_w(2)
            turn_w(3)
            pe.wait_ge(S["ld_ar"], 16 * (NB + 1))
            for k in range(NB):
                last = pe.transpose(p_x[:, E * k:E * k + E], router_rows[:, k * P:(k + 1) * P], ident[0:E, 0:E])
            last.then_inc(S["r_tr"], 1)
            pe.wait_ge(S["planes"], 1)
            for f in range(7):
                last = pe.transpose(p_a[:, f * P:(f + 1) * P], planes[:, f, :], ident)
            last.then_inc(S["planes_t"], 1)
            pe.wait_ge(S["k_back"], 16)
            pe.wait_ge(S["planes_c"], 1)
            for bank in range(2):
                last = pe.matmul(p_a[:, 512 * bank:512 * bank + 512], exch, t_rev[:, 512 * bank:512 * bank + 512],
                                 start=True, stop=True)
            last.then_inc(S["t_rev"], 1)
            turn_w(4)
            turn_w(5)
            pe.wait_ge(S["t_hi_s"], 1)
            pe.wait_ge(S["t_split"], 1)
            pe.wait_ge(S["consts_g"], 2)
            toeplitz(pe, lambda j: ones_r[:, :], None, p_a, "cum_mm")
            turn_w(6)
            turn_w(7)
            pe.wait_ge(S["r_evac"], 1)
            for k in range(NB):
                last = pe.matmul(p_x[:, 128:128 + AR], ones[:, :], ar_raw[:, k, :], start=(k == 0), stop=(k == NB - 1))
            last.then_inc(S["ar_mean"], 1)
            pe.wait_ge(S["cum_done"], 1)
            pe.wait_ge(S["ld_misc"], 80)
            pa = p_a[:, :].rearrange("p (h a c) -> p h a c", h=TH, a=NB)
            for h in range(TH):
                for k in range(NB):
                    last = pe.matmul(pa[:, h, k, :], cls_row[:, k * P:(k + 1) * P], ones[0:1, 0:C], start=True, stop=True)
            last.then_inc(S["h1T"], 1)
            pe.wait_ge(S["w_lo_s"], NB)
            pe.wait_ge(S["ar_done"], 2)
            pe.wait_ge(S["lb_done"], 1)

            def three(o, x_hi, x_lo, y_hi, y_lo, start, stop):
                pe.matmul(o, x_hi, y_hi, start=start, stop=False)
                pe.matmul(o, x_hi, y_lo, start=False, stop=False)
                return pe.matmul(o, x_lo, y_hi, start=False, stop=stop)

            def step(t, par, turn):
                n = t if isinstance(t, int) else None
                cur, feed, nxt = n is None or n <= TILES, n is None or n >= 1, n is None or n < TILES
                prv = 1 - par
                if nxt:
                    pe.wait_ge(S["x_sw"], t + 1)
                    if feed:
                        pe.wait_ge(S["g_prod"], t)
                if cur:
                    pe.wait_ge(S["h1hi"], t + 1)
                    pe.wait_ge(S["h1lo"], t + 1)
                    if feed:
                        pe.wait_ge(S["h2lo"], t)
                    for k in range(NB):
                        last = pe.transpose(p_b[:, k * P:(k + 1) * P], h1_t[:, k, :], ident)
                    last.then_inc(S["h1row"], 1)
                if nxt:
                    for h in range(TH):
                        pe.transpose(p_x[:, h * C:(h + 1) * C], x_in[:, prv, h, :], ident[0:C, 0:C])
                        last = pe.transpose(p_x[:, (TH + h) * C:(TH + h + 1) * C], x_swap[:, prv, h, :], ident[0:C, 0:C])
                    last.then_inc(S["x_t"], 1)
                if cur:
                    toeplitz(pe, lambda j: h1_hi[:, j, :], lambda j: h1_lo[:, j, :], p_a, "y_mm")
                if feed:
                    feed_forward(t, prv, 0, n)
                if cur:
                    pe.wait_ge(S["h2_s"], 2 * t + 2)
                    pe.wait_ge(S["h1_sb"], t + 1)
                    for k in range(NB):
                        last = pe.transpose(p_b[:, k * P:(k + 1) * P], h2[:, k * P:(k + 1) * P], ident)
                    last.then_inc(S["h2T"], 1)
                if nxt:
                    pe.wait_ge(S["g_split"], t + 1)
                    pe.wait_ge(S["q_split"], t + 1)
                    for h in range(TH):
                        g_of = [g[:, h, :, :].rearrange("p a c -> p (a c)") for g in (g_hi, g_lo)]
                        last = three(p_a[:, h * 512:(h + 1) * 512], q_hi[:, h, :], q_lo[:, h, :], *g_of, True, True)
                    last.then_inc(S["h1T"], 1)
                if feed:
                    feed_forward(t, prv, 1, n)
                    pe.wait_ge(S["gated"], t)
                    pe.transpose(p_x[:, 256:384], hw[:, :], ident).then_inc(S["hwT"], 1)
                    feed_forward(t, prv, 2, n)
                    pe.wait_ge(S["hw_split"], 2 * t)
                    for c in range(NC):
                        bank, w = product(c)
                        at = c * 512 + (AR if c == 0 else 0)
                        o = slice(w.start - AR if c else 0, w.stop - AR)
                        if c == 0:
                            pe.wait_ge(S["base0"], t)
                        three(p_f[:, at:bank.stop], hw_hi[:, :], hw_lo[:, :], lb_hi[:, o], lb_lo[:, o], c == 0, True)\
                            .then_inc(S["o_mm"], 1)

            def feed_forward(t, prv, c, n):
                if n is None or n >= 2:
                    pe.wait_ge(S["fin"], NC * (t - 2) + c + 1)
                bank, w = product(c)
                for k in range(NB):
                    last = three(p_f[:, bank], h2_hi[:, prv, k, :], h2_lo[:, prv, k, :], wa_hi[:, k, w], wa_lo[:, k, w],
                                 k == 0, c == 0 and k == NB - 1)
                if c == 0:
                    last.then_inc(S["ar_mm"], 1)

            steps(pe, step)

        @block.scalar
        def _(act):
            def mean_w(i):
                act.wait_ge(S[f"ld_w{i % 2}"], 16 * (i // 2 + 1))
                if i >= 2:
                    act.wait_ge(S["w_tr"], i - 1)
                act.activation(h2_bias[:, i % 2, :], res[:, i % 2, :], ACT.Copy, scale=-1.0 / L,
                               accum_out=w_mean[:, i:i + 1]).then_inc(S["w_mean"], 1)

            def turned(i):
                return w_turned[i % 2].rearrange("p (k o) -> p k o", k=NB)

            def high_w(i):
                act.wait_ge(S["w_tr"], i + 1)
                act.activation(wa_hi[:, :, AR + i * P:AR + (i + 1) * P], turned(i), ACT.Copy).then_inc(S["w_hi_s"], 1)

            act.wait_ge(S["s4_d"], 1)
            act.activation(s4_sin, h1[:, :], ACT.Square).then_inc(S["s4_sq"], 1)
            act.activation(s4_cos, h2[:, :], ACT.Square).then_inc(S["s4_sq"], 1)
            mean_w(0)
            mean_w(1)
            act.wait_ge(S["ld_const"], 16)
            act.activation(ident_r[:, :], ident, ACT.Copy).then_inc(S["consts_g"], 1)
            act.wait_ge(S["p_chain"], 1)
            act.activation(ones_r[:, :], ones[:, :], ACT.Copy).then_inc(S["consts_g"], 1)
            high_w(0)
            high_w(1)
            mean_w(2)
            mean_w(3)
            act.wait_ge(S["ssm_r"], 1)
            act.activation(sm(27), sm(26), ACT.Sin).then_inc(S["ssm_s"], 1)
            act.activation(sm(25), sm(26), ACT.Sin, scale=0.5).then_inc(S["ssm_s"], 1)
            for i in (2, 3):
                high_w(i)
                mean_w(i + 2)
            act.wait_ge(S["t_rev"], 1)
            act.activation(t_hi[:, :], p_a[:, :], ACT.Copy).then_inc(S["t_hi_s"], 1)
            for i in (4, 5):
                high_w(i)
                mean_w(i + 2)
            act.wait_ge(S["ld_misc"], 80)
            act.activation(lb_hi[:, :], lora_b, ACT.Copy).then_inc(S["lb_hi_s"], 1)
            act.wait_ge(S["size_e"], 1)
            act.activation(size_flat, size_flat, ACT.Exp).then_inc(S["size_done"], 1)
            act.wait_ge(S["cum_mm"], 2)
            act.wait_ge(S["lb_done"], 1)
            act.activation(neg_cum[:, :], p_a[:, :], ACT.Copy, scale=-1.0).then_inc(S["cum_done"], 1)
            high_w(6)
            high_w(7)
            act.wait_ge(S["ar_cent"], 1)
            act.activation(wa_hi[:, :, 0:AR], ar_raw, ACT.Copy).then_inc(S["ar_done"], 1)

            def waves(t):
                act.wait_ge(S["angles"], t)
                if isinstance(t, int) and t == 1:
                    pass
                else:
                    act.wait_ge(S["power_done"], t - 1)
                act.activation(wave[:, :, :, :], angle[:, :, :, :], ACT.Sin, scale=TWO_PI).then_inc(S["waves"], 1)

            def high_q(t):
                act.wait_ge(S["q_done"], t)
                act.activation(q_hi[:, :, :], q_a[:, :, :], ACT.Copy).then_inc(S["q_hi_s"], 1)

            def high_g(t):
                act.wait_ge(S["g_done"], t)
                act.activation(flat(g_hi), flat(g_a), ACT.Copy).then_inc(S["g_hi_s"], 1)

            def take_h1(t):
                act.wait_ge(S["h1T"], t + 1)
                act.activation(by_head(h1_t), by_head_psum, ACT.Copy).then_inc(S["h1_t"], 1)
                act.wait_ge(S["h1_t"], t + 1)
                act.activation(h1_hi[:, :, :], h1_t[:, :, :], ACT.Copy).then_inc(S["h1hi"], 1)

            waves(1)
            high_q(1)
            take_h1(0)

            def step(t, par, turn):
                n = t if isinstance(t, int) else None
                cur, feed, nxt = n is None or n <= TILES, n is None or n >= 1, n is None or n < TILES
                if cur:
                    act.wait_ge(S["h1row"], t + 1)
                    if feed:
                        act.wait_ge(S["h2_s"], 2 * t)
                    act.activation(h1[:, :], p_b[:, :], ACT.Copy).then_inc(S["h1_sb"], 1)
                if nxt:
                    high_g(t + 1)
                if cur:
                    act.wait_ge(S["h2T"], t + 1)
                    act.activation(h2_hi[:, par, :, :].rearrange("p k c -> p (k c)"), p_b[:, :], ACT.Copy).then_inc(S["h2hi"], 1)
                if nxt:
                    take_h1(t + 1)
                if feed:
                    act.wait_ge(S["hwT"], t)
                    if n is None or n >= 2:
                        act.wait_ge(S["o_mm"], NC * (t - 1))
                    act.activation(hw_hi[:, :], p_x[:, 256:384], ACT.Copy).then_inc(S["hw_split"], 1)
                if n is None or n < TILES - 1:
                    waves(t + 2)
                    high_q(t + 2)

            steps(act, step)

        @block.gpsimd
        def _(pool):
            pool.memset(ones[:, :], 1.0).then_inc(S["p_chain"], 1)
            pool.memset(zero_row[:, :], 0.0).then_inc(S["p_chain"], 1)
            pool.memset(minus_half[:, :], -0.5).then_inc(S["p_chain"], 1)
            pool.memset(eps[:, :], EPS).then_inc(S["p_chain"], 1)
            for i in range(NB):
                if i == 6:
                    pool.wait_ge(S["planes_c"], 1)
                    pool.wait_ge(S["s4_ktc"], 1)
                    pool.tensor_tensor(size[:, :, :], bcast(planes_t[:, 0, :], 2, PW), bcast(powers[:, 0:PW], 1, H), ALU.mult)\
                        .then_inc(S["size_e"], 1)
                pool.wait_ge(S["w_mean"], i + 1)
                pool.tensor_scalar(h2_bias[:, i % 2, :], res[:, i % 2, :], w_mean[:, i:i + 1], 1.0, ALU.add, ALU.mult)\
                    .then_inc(S["w_cent"], 1)
            def swap(par):
                for r in range(2):
                    ins = pool.tensor_copy(x_swap[:, par, :, r::2], x_in[:, par, :, 1 - r::2])
                ins.then_inc(S["x_sw"], 1)

            own = step_chain(pool, "g_step")

            def turns_low(t):
                pool.tensor_tensor(turn_l[:, :, :], bcast(planes_t[:, 2, heads(t)], 2, PW), bcast(powers[:, 0:PW], 1, TH), ALU.mult)\
                    .then_inc(S["turn_low"], 1)

            def make_powers(t, par):
                pool.wait_ge(S["waves"], t)
                own(pool.tensor_tensor(power[:, par, :, :, :], wave[:, :, :, :], bcast(size[:, heads(t), :], 1, 2), ALU.mult))
                own.wait()
                for k in range(2):
                    f = 3 + 2 * k
                    own(pool.tensor_tensor(uw_prod[:, k, :, :, :], power[:, par, :, :, 0:NB],
                                           bcast(planes_t[:, f:f + 2, heads(t)], 3, NB), ALU.mult))
                own.wait()
                last = pool.tensor_tensor(uw[:, par, :, :, :], uw_prod[:, :, 0, :, :], uw_prod[:, :, 1, :, :], ALU.add)
                last.then_inc(S["power_done"], 1)

            def make_q(par):
                z16 = [power[:, par, k, :, NB:NB + NE] for k in range(2)]
                z1_sin, z1_cos = (power[:, par, k, :, NB + NE:PW] for k in range(2))
                for q, x, y in ((q_a, z16[0], z1_cos), (q_b, z16[1], z1_sin)):
                    own(pool.tensor_tensor(q[:, :, :].rearrange("p h (i j) -> p h i j", i=NE), bcast(x, 3, NF), bcast(y, 2, NE), ALU.mult))
                own.wait()
                pool.tensor_tensor(q_a[:, :, :], q_a[:, :, :], q_b[:, :, :], ALU.add).then_inc(S["q_done"], 1)

            def step(t, par, turn):
                n = t if isinstance(t, int) else None
                cur, feed, nxt = n is None or n <= TILES, n is None or n >= 1, n is None or n < TILES
                prv = 1 - par
                own.start()
                if nxt:
                    pool.wait_ge(S["q_hi_s"], t + 1)
                    pool.wait_ge(S["h1T"], t + 1)
                    if n is None or n < TILES - 1:
                        pool.wait_ge(S["angles"], t + 1)
                    pool.tensor_tensor(q_lo[:, :, :], q_a[:, :, :], q_hi[:, :, :].bitcast(F32), ALU.subtract).then_inc(S["q_split"], 1)
                if n is None or n < TILES - 1:
                    turns_low(t + 2)
                if nxt:
                    pool.wait_ge(S["g_prod"], t + 1)
                    pool.tensor_tensor(flat(g_a), flat(g_a), flat(g_b), ALU.add).then_inc(S["g_done"], 1)
                if cur:
                    pool.wait_ge(S["mvar1"], t + 1)
                    if feed:
                        pool.wait_ge(S["h2_s"], 2 * t)
                    own(pool.tensor_tensor(v_eps[:, 0:1], mv1[:, 1:2], eps[:, :], ALU.add))
                    own.wait()
                    pool.tensor_tensor(rstd1[:, :], v_eps[:, 0:1], minus_half[:, :], ALU.pow).then_inc(S["rs1"], 1)
                if nxt:
                    pool.wait_ge(S["g_hi_s"], t + 1)
                    if n is None or n < TILES - 1:
                        if n is None or n >= 1:
                            pool.wait_ge(S["x_t"], t)
                        pool.wait_ge(S[f"ld_x{par}"], 16 * (turn + 2))
                    pool.tensor_tensor(flat(g_lo), flat(g_a), flat(g_hi).bitcast(F32), ALU.subtract).then_inc(S["g_split"], 1)
                if n is None or n < TILES - 1:
                    swap(par)
                if cur:
                    pool.wait_ge(S["h2_s"], 2 * t + 2)
                    if n is None or n >= 2:
                        pool.wait_ge(S["fin"], NC * (t - 1))
                    pool.tensor_tensor(h2_bias[:, par, :], h2[:, :], bias[:, :], ALU.add).then_inc(S["h2b"], 1)
                    pool.wait_ge(S["mvar2"], t + 1)
                    own(pool.tensor_tensor(v_eps[:, 1:2], mv2[:, 1:2], eps[:, :], ALU.add))
                    own.wait()
                    pool.tensor_tensor(rstd2[:, par, :], v_eps[:, 1:2], minus_half[:, :], ALU.pow).then_inc(S["rs2"], 1)
                if n is None or n < TILES - 1:
                    make_powers(t + 2, par)
                    make_q(par)

            pool.wait_ge(S["ld_x1"], 16)
            swap(1)
            pool.wait_ge(S["size_done"], 1)
            own.start()
            turns_low(1)
            make_powers(1, 1)
            make_q(1)
            steps(pool, step)

        @block.vector
        def _(dve):
            link = chain(dve, "v_chain")

            def ts(o, i, s1, s2=None, op0=ALU.mult, op1=None):
                link(dve.tensor_scalar(o, i, s1, s2, op0, op1) if op1 is not None else dve.tensor_scalar(o, i, s1, None, op0))

            def tt(o, x, y, op):
                link(dve.tensor_tensor(o, x, y, op))

            def stt(o, x, s, y, op0=ALU.mult, op1=ALU.add):
                link(dve.scalar_tensor_tensor(out=o, in0=x, scalar=s, in1=y, op0=op0, op1=op1))

            def copy(o, i):
                link(dve.tensor_copy(o, i))

            mul, add, sub = ALU.mult, ALU.add, ALU.subtract

            def exp_parts(x, w, k, r, p, two):
                ts(k, x, 1.4426950408889634, MAGIC, mul, add)
                ts(k, k, -MAGIC, -126.0, add, ALU.max)
                stt(r, k, -LN2_PARTS[0], x)
                stt(r, k, -LN2_PARTS[1], r)
                series = exp_series()
                ts(p, r, series[0])
                for c in series[1:]:
                    stt(p, p, c, r, add, mul)
                ts(k, k, 127.0, 127.0, ALU.min, add)
                ts(two.bitcast(I32), k, float(2 ** 23))

            dve.wait_ge(S["ld_exp"], 48)
            w = N + 2
            x0, k, r, p, two, ex = (sm(n, w) for n in (0, 13, 14, 15, 16, 2))
            exp_parts(x0, w, k, r, p, two)
            stt(ex, p, 1.0, two, add, mul)
            ea, dt, stp = ex[:, 0:N], ex[:, N:N + 1], ex[:, N + 1:N + 2]

            dve.wait_ge(S["ld_s4"], 16 * 13)
            lam = small[:, 4, 0:2]
            sv = small[:, 16, 0:4].rearrange("p (v r) -> p v r", v=2)
            prod = small[:, 17:19, 0:N]
            tt(prod, vc.rearrange("p n r -> p r n"), bcast(sm(7), 1, 2), mul)
            link(dve.tensor_reduce(sv[:, 0, :], prod, AX.X, add))
            copy(sv[:, 1, :], small[:, 4, 4:6])
            vv = small[:, 17, 0:8].rearrange("p (m v r) -> p m v r", m=2, v=2)
            t2 = small[:, 18, 0:2]
            for m, at in enumerate((2, 6)):
                mr, mi = small[:, 4, at:at + 1], small[:, 4, at + 1:at + 2]
                ts(t2, sv[:, :, 0], mr)
                stt(vv[:, m, :, 0], sv[:, :, 1], mi, t2)
                ts(t2, sv[:, :, 0], mi)
                stt(vv[:, m, :, 1], sv[:, :, 1], mr, t2, mul, sub)
            vm = small[:, 31, 0:8].rearrange("p (j r) -> p j r", r=2)
            vj = small[:, 17, 0:8].rearrange("p (j r) -> p j r", r=2)
            copy(vm[0:N], vj[0:N])
            ts(vm[N:P, :, 0], vj[N:P, :, 1], -1.0)
            copy(vm[N:P, :, 1], vj[N:P, :, 0])
            g2, nl = small[:, 19, 0:1], small[:, 19, 2:4]
            link(dve.reciprocal(g2, stp))
            ts(g2, g2, 2.0)
            ts(nl, lam, -1.0)
            ts(h1[:, :], s4_cos, nl[:, 0:1])
            ts(h2[:, :], s4_sin, g2)
            dve.scalar_tensor_tensor(out=h2[:, :], in0=s4_cos, scalar=nl[:, 1:2], in1=h2[:, :], op0=mul, op1=add)\
                .then_inc(S["s4_d"], 1)
            dve.wait_ge(S["s4_sq"], 2)
            tt(s4_sin, s4_sin, s4_cos, add)
            link(dve.reciprocal(s4_cos, s4_sin))
            tt(h1[0:N, :], h1[0:N, :], s4_cos[0:N, :], mul)
            stt(h1[N:P, :], h2[N:P, :], -1.0, s4_cos[N:P, :], mul, mul)
            dve.sem_inc(S["s4_v"], 1)

            def low_w(i):
                dve.wait_ge(S["w_hi_s"], i + 1)
                cols = slice(AR + i * P, AR + (i + 1) * P)
                dve.tensor_tensor(wa_lo[:, :, cols], w_turned[i % 2].rearrange("p (k o) -> p k o", k=NB),
                                  wa_hi[:, :, cols].bitcast(F32), sub).then_inc(S["w_lo_s"], 1)

            dve.wait_ge(S["s4_sum"], 1)
            dve.wait_ge(S["ld_s4b"], 64)
            sums = small[:, 16, 0:N]
            copy(sums, p_s[:, 0:N])
            s = sums.rearrange("p (q j) -> p j q", q=NB)
            c8, s8 = sm(8, NB), sm(9, NB)
            tr, ti, den, tmp, xr, xi, yr, yi = (sm(n, NB) for n in (17, 18, 19, 20, 21, 22, 23, 24))
            tt(tr, c8, s[:, 6], mul)
            ts(tr, tr, 1.0, None, add)
            tt(ti, c8, s[:, 7], mul)
            tt(den, tr, tr, mul)
            tt(tmp, ti, ti, mul)
            tt(den, den, tmp, add)
            link(dve.reciprocal(den, den))
            tt(xr, s[:, 2], s[:, 4], mul)
            tt(tmp, s[:, 3], s[:, 5], mul)
            tt(xr, xr, tmp, sub)
            tt(xr, xr, c8, mul)
            tt(xi, s[:, 2], s[:, 5], mul)
            tt(tmp, s[:, 3], s[:, 4], mul)
            tt(xi, xi, tmp, add)
            tt(xi, xi, c8, mul)
            tt(yr, xr, tr, mul)
            tt(tmp, xi, ti, mul)
            tt(yr, yr, tmp, add)
            tt(yr, yr, den, mul)
            tt(yi, xi, tr, mul)
            tt(tmp, xr, ti, mul)
            tt(yi, yi, tmp, sub)
            tt(yi, yi, den, mul)
            tt(yr, s[:, 0], yr, sub)
            tt(yi, s[:, 1], yi, sub)
            at1, at2 = small[:, 29, 0:2 * NB], small[:, 30, 0:2 * NB]
            tt(xr, c8, yr, mul)
            tt(tmp, s8, yi, mul)
            tt(at1[:, 0:NB], xr, tmp, sub)
            tt(xr, c8, yi, mul)
            tt(tmp, s8, yr, mul)
            tt(at1[:, NB:], xr, tmp, add)
            ts(at2[:, 0:NB], at1[:, NB:], -1.0)
            copy(at2[:, NB:], at1[:, 0:NB])
            dve.sem_inc(S["s4_at"], 1)
            low_w(0)
            dve.wait_ge(S["s4_b"], 1)
            kp = small[:, 18:20, 0:N].rearrange("p a b -> p a b")
            spec = sm(17, 2 * NB)
            copy(spec, p_s[:, 64:80])
            tw = twiddle.rearrange("p (r q) -> p r q", r=NB)
            tt(tw, tw, bcast(spec, 1, NB), mul)
            kern = sm(28, NB)
            link(dve.tensor_reduce(kern, tw, AX.X, add))
            tt(kern[0:1, 0:1], kern[0:1, 0:1], small[0:1, 10, 0:1], add)
            dve.sem_inc(S["s4_k"], 1)
            dve.wait_ge(S["s4_kt"], 1)
            dve.tensor_copy(k_rows, p_s[0:NB, 128:256]).then_inc(S["s4_ktc"], 1)
            low_w(1)

            dve.wait_ge(S["ld_ssm"], 48)
            a_im, alpha, om = sm(1), sm(18), sm(19)
            ts(alpha, ea, dt, -1.0, mul, mul)
            ts(om, a_im, dt)
            k, r, p, two, em1 = (sm(n) for n in (13, 14, 15, 16, 20))
            exp_parts(alpha, N, k, r, p, two)
            tt(p, two, p, mul)
            stt(em1, two, -1.0, p, add, add)
            ts(k, om, INV_2PI, MAGIC, mul, add)
            ts(k, k, -MAGIC, None, add)
            phase = sm(26)
            stt(phase, k, -PI_PARTS[0], om)
            stt(phase, k, -PI_PARTS[1], phase)
            stt(phase, k, -PI_PARTS[2], phase)
            dve.tensor_scalar(phase, phase, 3.1415925, -3.1415925, ALU.min, ALU.max).then_inc(S["ssm_r"], 1)
            dve.wait_ge(S["ssm_r"], 1)
            turns, turns_h, turns_l = sm(21), sm(22), sm(23)
            ts(turns, phase, INV_2PI)
            ts(turns_h, turns, MAGIC13, -MAGIC13, add, add)
            tt(turns_l, turns, turns_h, sub)
            dve.wait_ge(S["ssm_s"], 2)
            s1, s2 = sm(27), sm(25)
            er, ei = sm(13), sm(14)
            tt(s2, s2, s2, mul)
            ts(er, s2, -2.0, 1.0, mul, add)
            tt(er, er, em1, mul)
            stt(er, s2, -2.0, er)
            stt(ei, em1, 1.0, s1, add, mul)
            den, tmp, nr, ni = sm(15), sm(16), sm(18 + 6), sm(12)
            tt(den, a_im, a_im, mul)
            tt(tmp, ea, ea, mul)
            tt(den, den, tmp, add)
            link(dve.reciprocal(den, den))
            tt(nr, ei, a_im, mul)
            tt(tmp, er, ea, mul)
            tt(nr, nr, tmp, sub)
            tt(ni, er, a_im, mul)
            tt(tmp, ei, ea, mul)
            tt(ni, ni, tmp, add)
            stt(nr, nr, 2.0, den, mul, mul)
            stt(ni, ni, 2.0, den, mul, mul)
            cr, ci = sm(13), sm(14)
            br, bi = ssm_b[:, :, 0], ssm_b[:, :, 1]
            tt(cr, nr, br, mul)
            tt(tmp, ni, bi, mul)
            tt(cr, cr, tmp, add)
            tt(ci, nr, bi, mul)
            tt(tmp, ni, br, mul)
            tt(ci, ci, tmp, sub)
            pv = planes.rearrange("p f (n r) -> p f n r", r=2)
            for f, t in ((0, alpha), (1, turns_h), (2, turns_l)):
                dve.tensor_copy(pv[:, f], bcast(t, 2, 2)).then_inc(S["pl"], 1)
            for f, even, odd in ((3, (cr, 1.0), (ci, 1.0)), (4, (ci, 1.0), (cr, -1.0)),
                                 (5, (ci, -1.0), (cr, -1.0)), (6, (cr, 1.0), (ci, -1.0))):
                for half, (t, sign) in enumerate((even, odd)):
                    dve.tensor_scalar(pv[:, f, :, half], t, sign, None, mul).then_inc(S["pl"], 1)
            dve.wait_ge(S["pl"], 11)
            copy(tmp, cr)
            dve.sem_inc(S["planes"], 1)

            low_w(2)
            dve.wait_ge(S["r_tr"], 1)
            dve.tensor_copy(ar_raw[:, :, ER:AR], p_x[:, 0:NB * E].rearrange("p (k e) -> p k e", k=NB)).then_inc(S["r_evac"], 1)
            dve.wait_ge(S["planes_t"], 1)
            dve.tensor_copy(planes_t[:, :, :].rearrange("p f h -> p (f h)"), p_a[:, 0:7 * P]).then_inc(S["planes_c"], 1)
            low_w(3)
            dve.wait_ge(S["t_hi_s"], 1)
            dve.tensor_tensor(t_lo[:, :], p_a[:, :], t_hi[:, :].bitcast(F32), sub).then_inc(S["t_split"], 1)
            low_w(4)
            low_w(5)
            dve.wait_ge(S["lb_hi_s"], 1)
            dve.tensor_tensor(lb_lo[:, :], lora_b, lb_hi[:, :].bitcast(F32), sub).then_inc(S["lb_done"], 1)
            low_w(6)
            low_w(7)
            dve.wait_ge(S["ar_mean"], 1)
            dve.scalar_tensor_tensor(out=ar_raw, in0=bcast(p_x[:, 128:128 + AR], 1, NB), scalar=-1.0 / L, in1=ar_raw,
                                     op0=mul, op1=add).then_inc(S["ar_cent"], 1)
            dve.wait_ge(S["ar_done"], 1)
            dve.tensor_tensor(wa_lo[:, :, 0:AR], ar_raw, wa_hi[:, :, 0:AR].bitcast(F32), sub).then_inc(S["ar_done"], 1)

            own = step_chain(dve, "v_step")

            def then(ins):
                own(ins)
                own.wait()

            def phases(t):
                hs = heads(t)
                then(dve.tensor_tensor(turn_f[:, :, :], bcast(planes_t[:, 1, hs], 2, PW), bcast(powers[:, 0:PW], 1, TH), mul))
                then(dve.tensor_tensor(turn_f[:, :, :], turn_f[:, :, :], bcast(powers[:, PW:2 * PW], 1, TH), add))
                dve.wait_ge(S["turn_low"], t)
                then(dve.tensor_tensor(turn_k[:, :, :], turn_f[:, :, :], turn_l[:, :, :], add))
                then(dve.tensor_scalar(turn_k[:, :, :], turn_k[:, :, :], MAGIC, -MAGIC, add, add))
                then(dve.tensor_tensor(turn_f[:, :, :], turn_f[:, :, :], turn_k[:, :, :], sub))
                if not (isinstance(t, int) and t == 1):
                    dve.wait_ge(S["waves"], t - 1)
                then(dve.tensor_tensor(angle[:, 0, :, :], turn_f[:, :, :], turn_l[:, :, :], add))
                then(dve.tensor_scalar(turn_k[:, :, :], angle[:, 0, :, :], 0.25, None, ALU.is_gt))
                dve.scalar_tensor_tensor(out=angle[:, 1, :, :], in0=angle[:, 0, :, :], scalar=0.25, in1=turn_k[:, :, :],
                                         op0=add, op1=sub).then_inc(S["angles"], 1)

            def stats(src, s):
                for half in range(2):
                    ins = dve.bn_stats(st[:, s, half, :], src[:, 512 * half:512 * half + 512])
                own(ins)

            def aggregate(s, mv, name):
                own.wait()
                dve.bn_aggr(mv[:, :], st[:, s, :, :].rearrange("p a b -> p (a b)")).then_inc(S[name], 1)

            def products(t, par):
                dve.wait_ge(S["x_t"], t)
                dve.wait_ge(S["power_done"], t)
                for k, g in enumerate((g_a, g_b)):
                    x = p_x[:, k * TH * C:(k + 1) * TH * C].rearrange("p (h c) -> p h c", h=TH)
                    ins = dve.tensor_tensor(g[:, :, :, :], bcast(x, 2, NB), bcast(uw[:, par, k, :, :], 3, C), mul)
                ins.then_inc(S["g_prod"], 1)

            def gate_step(prv):
                then(dve.scalar_tensor_tensor(out=logit[:, :], in0=p_f[:, ER:AR], scalar=rstd2[:, prv, :], in1=b_router[:, :],
                                              op0=mul, op1=add))
                then(dve.max(top[:, :], logit[:, :]))
                then(dve.tensor_tensor(top_sums[:, :, :], sparse[:, 0:E * E].rearrange("p (k i) -> p k i", k=E),
                                       bcast(top[:, :], 1, E), mul))
                then(dve.tensor_reduce(tau[:, :], top_sums[:, :, :], AX.X, add))
                then(dve.tensor_tensor(tau[:, :], tau[:, :], sparse[:, E * E:E * E + E], add))
                then(dve.tensor_reduce(tau1[:, :], tau[:, :], AX.X, ALU.max))
                then(dve.tensor_scalar(gate[:, :], logit[:, :], tau1[:, :], 0.0, sub, ALU.max))
                dve.tensor_tensor(hw[:, :].rearrange("p (e r) -> p e r", e=E), p_f[:, 0:ER].rearrange("p (e r) -> p e r", e=E),
                                  bcast(gate[:, :], 2, RK), mul).then_inc(S["gated"], 1)

            def finish(prv, c, gated=True):
                at = 512 * c + (AR if c == 0 else 0)
                cols = slice(max(CUTS[c] - AR, 0), CUTS[c + 1] - AR)
                plus = res if c == 0 and gated else h2_bias
                return dve.scalar_tensor_tensor(out=res[:, prv, cols], in0=p_f[:, at:512 * c + CUTS[c + 1] - CUTS[c]],
                                                scalar=rstd2[:, prv, :], in1=plus[:, prv, cols], op0=mul, op1=add)

            def low_h1(t):
                dve.wait_ge(S["h1hi"], t + 1)
                dve.tensor_tensor(h1_lo[:, :, :], h1_t[:, :, :], h1_hi[:, :, :].bitcast(F32), sub).then_inc(S["h1lo"], 1)

            def step(t, par, turn):
                n = t if isinstance(t, int) else None
                cur, feed, nxt = n is None or n <= TILES, n is None or n >= 1, n is None or n < TILES
                prv = 1 - par
                own.start()
                if nxt:
                    if feed:
                        dve.wait_ge(S["g_split"], t)
                    products(t + 1, prv)
                if cur:
                    dve.wait_ge(S["h1_sb"], t + 1)
                    stats(h1, 0)
                    aggregate(0, mv1, "mvar1")
                if cur and feed:
                    dve.wait_ge(S["h2T"], t)
                    dve.wait_ge(S["h2b"], t)
                    dve.wait_ge(S["rs2"], t)

                def centre(half):
                    cols = slice(512 * half, 512 * half + 512)
                    dve.wait_ge(S["y_mm"], 2 * t + 1 + half)
                    own(dve.scalar_tensor_tensor(out=h2[:, cols], in0=neg_cum[:, cols], scalar=mv1[:, 0:1], in1=p_a[:, cols],
                                                 op0=mul, op1=add))
                if cur:
                    dve.wait_ge(S["mvar1"], t + 1)
                    centre(0)
                if n is None or n < TILES - 1:
                    phases(t + 2)
                if cur:
                    centre(1)
                    dve.wait_ge(S["rs1"], t + 1)
                    for half in range(2):
                        cols = slice(512 * half, 512 * half + 512)
                        if half == 0:
                            own.wait()
                        dve.scalar_tensor_tensor(out=h2[:, cols], in0=h2[:, cols], scalar=rstd1[:, :], in1=h1[:, cols],
                                                 op0=mul, op1=add).then_inc(S["h2_s"], 1)
                    dve.wait_ge(S["h2_s"], 2 * t + 2)
                    stats(h2, 1)
                    aggregate(1, mv2, "mvar2")
                if feed:
                    dve.wait_ge(S["ar_mm"], t)
                    if not cur:
                        dve.wait_ge(S["rs2"], t)
                    gate_step(prv)
                    if n is None or n >= 3:
                        dve.wait_ge(S[f"stored{prv}"], 32 * turn - 16 * par)
                    finish(prv, 0, False).then_inc(S["base0"], 1)
                if cur:
                    dve.wait_ge(S["h2hi"], t + 1)
                    dve.tensor_tensor(h2_lo[:, par, :, :].rearrange("p k c -> p (k c)"), p_b[:, :],
                                      h2_hi[:, par, :, :].rearrange("p k c -> p (k c)").bitcast(F32), sub).then_inc(S["h2lo"], 1)
                if nxt:
                    low_h1(t + 1)
                if feed:
                    dve.wait_ge(S["hw_split"], 2 * t - 1)
                    dve.tensor_tensor(hw_lo[:, :], p_x[:, 256:384], hw_hi[:, :].bitcast(F32), sub).then_inc(S["hw_split"], 1)
                    for c in range(NC):
                        dve.wait_ge(S["o_mm"], NC * (t - 1) + 1 + c)
                        finish(prv, c).then_inc(S["fin"], 1)

            own.start()
            phases(1)
            low_h1(0)
            steps(dve, step)


_INS = ["x", "cls_tok", "L0_tok_log_dt", "L0_tok_B", "L0_tok_inv_A_real", "L0_tok_A_imag", "L0_attn_Lambda_ri",
        "L0_attn_p_ri", "L0_attn_q_ri", "L0_attn_Vc_ri", "L0_attn_Ct_ri", "L0_attn_Bp", "L0_attn_D",
        "L0_attn_log_step", "L0_ffn_W_base", "L0_ffn_b_base", "L0_ffn_W_router", "L0_ffn_b_router",
        "L0_ffn_lora_A", "L0_ffn_lora_B"]


def kernel(**inputs):
    import concourse.bacc as _bacc
    from concourse.bass_utils import run_bass_kernel_spmd as _run

    nc = _bacc.Bacc("TRN2", target_bir_lowering=False, num_devices=1)
    arrays = {name: np.ascontiguousarray(inputs[name]) for name in _INS}
    arrays.update(shape_tables())
    aps = {name: nc.dram_tensor(f"in_{name}", x.shape, mybir.dt.from_np(x.dtype), kind="ExternalInput").ap()
           for name, x in arrays.items()}
    out = nc.dram_tensor("out_0", (C, H + 1, L), F32, kind="ExternalOutput").ap()
    build(nc, aps, out)
    r = _run(nc, [{f"in_{name}": x for name, x in arrays.items()}], core_ids=[0])
    return r.results[0]["out_0"]
```

```python
from contextlib import ExitStack

import numpy as np

import concourse.bass as bass
from concourse import mybir

F32 = mybir.dt.float32
F32R = mybir.dt.float32r
I32 = mybir.dt.int32
ALU = mybir.AluOpType
ACT = mybir.ActivationFunctionType
AX = mybir.AxisListType

P = 128
C = 64
H = 128
N = 64
L = 1024
NB = L // P
E = 8
RK = 16
ER = E * RK
AR = ER + E
WA = AR + L
CUTS = (0, 386, 774, WA)
NC = len(CUTS) - 1
TH = P // C
TILES = H // TH
NE, NF = 8, 16
PW = NB + NE + NF
EPS = 1e-5
MAGIC = 12582912.0
MAGIC13 = 1536.0
TWO_PI = float(np.float32(6.2831850))
INV_2PI = 0.15915494309189535
PI_PARTS = (6.28125, 0.0019350051879882812, 3.0198490e-07)
LN2_PARTS = (0.693359375, -2.12194440e-4)


def exp_series():
    out, f = [], 1.0
    for k in range(1, 9):
        f *= k
        out.append(1.0 / f)
    return out[::-1]


def shape_tables():
    f = np.float32
    ident = np.eye(P, dtype=f)
    power = np.concatenate([128 * np.arange(NB), 16 * np.arange(NE), np.arange(NF)])
    phase = np.zeros((P, PW))
    phase[0::2, 0:NB + NE] = 0.25
    powers = np.concatenate([np.broadcast_to(power, (P, PW)), phase], 1).astype(f)
    half = np.pi * np.arange(L) / L
    half = np.stack([np.cos(half), np.sin(half)]).astype(f)
    ps = 2 * np.pi * np.outer(np.arange(P), np.arange(P)) / P
    r, s, q = np.arange(NB), np.arange(P), np.arange(NB)
    ang = 2 * np.pi * q[None, None, :] * (128 * r[None, :, None] + s[:, None, None]) / L
    twiddle = np.concatenate([np.cos(ang), -np.sin(ang)], 2) / L
    k = np.arange(1, E + 1)
    mean_of_top = np.tril(np.ones((E, E))) / k[:, None]
    sparse = np.concatenate([mean_of_top.ravel(), -1.0 / k])
    return {
        "k_ident": np.concatenate([ident, ident[::-1], np.cos(ps), np.sin(ps)], 1).astype(f),
        "k_powers": powers,
        "k_half": half,
        "k_twiddle": twiddle.reshape(P, NB * 2 * NB).astype(f),
        "k_sparse": np.broadcast_to(sparse, (P, E * E + E)).astype(f).copy(),
    }


def raw(t, offset, dims):
    return bass.AP(tensor=t.tensor, offset=offset, ap=[list(d) for d in dims])


def build(nc, a, out, dbg=None):
    with ExitStack() as ctx:
        def sb(name, shape, dt=F32):
            return ctx.enter_context(nc.sbuf_tensor(name, shape, dt))

        def sem(name):
            return ctx.enter_context(nc.semaphore(name))

        def psum(name, n):
            return ctx.enter_context(nc.psum_tensor(name, [P, n], F32))

        ident4 = sb("ident4", [P, 4 * P])
        ident, exch = ident4[:, 0:P], ident4[:, P:2 * P]
        dft_cos, dft_sin = ident4[:, 2 * P:3 * P], ident4[:, 3 * P:4 * P]
        ident_r, ones_r = sb("ident_r", [P, P], F32R), sb("ones_r", [P, P], F32R)
        ones = sb("ones", [P, P])
        wa_hi, wa_lo = sb("wa_hi", [P, NB, WA], F32R), sb("wa_lo", [P, NB, WA], F32R)
        lb_hi, lb_lo = sb("lb_hi", [P, L], F32R), sb("lb_lo", [P, L], F32R)
        t_hi, t_lo = sb("t_hi", [P, L], F32R), sb("t_lo", [P, L], F32R)
        neg_cum = sb("neg_cum", [P, L])
        bias = sb("bias", [P, L])
        b_router = sb("b_router", [P, E])
        sparse = sb("sparse", [P, E * E + E])
        planes_t = sb("planes_t", [P, 7, P])
        size = sb("size", [P, H, PW])
        powers = sb("powers", [P, 2 * PW])
        x_in = sb("x_in", [C, 2, TH, P])
        x_swap = sb("x_swap", [C, 2, TH, P])
        turn_f, turn_l, turn_k = (sb(n, [P, TH, PW]) for n in ("turn_f", "turn_l", "turn_k"))
        angle, wave = sb("angle", [P, 2, TH, PW]), sb("wave", [P, 2, TH, PW])
        power = sb("power", [P, 2, 2, TH, PW])
        uw_prod, uw = sb("uw_prod", [P, 2, 2, TH, NB]), sb("uw", [P, 2, 2, TH, NB])
        g_a, g_b = sb("g_a", [P, TH, NB, C]), sb("g_b", [P, TH, NB, C])
        g_hi, g_lo = sb("g_hi", [P, TH, NB, C], F32R), sb("g_lo", [P, TH, NB, C], F32R)
        q_a, q_b = sb("q_a", [P, TH, P]), sb("q_b", [P, TH, P])
        q_hi, q_lo = sb("q_hi", [P, TH, P], F32R), sb("q_lo", [P, TH, P], F32R)
        h1_t = sb("h1_t", [P, NB, P])
        h1_hi, h1_lo = sb("h1_hi", [P, NB, P], F32R), sb("h1_lo", [P, NB, P], F32R)
        h1, h2 = sb("h1", [P, L]), sb("h2", [P, L])
        h2_hi = sb("h2_hi", [P, 2, NB, P], F32R)
        h2_lo = sb("h2_lo", [P, 2, NB, P], F32R)
        h2_bias = sb("h2_bias", [P, 2, L])
        res = sb("res", [P, 2, L])
        st = sb("st", [P, 2, 2, 6])
        mv1, mv2 = sb("mv1", [P, 2]), sb("mv2", [P, 2])
        rstd1, rstd2 = sb("rstd1", [P, 1]), sb("rstd2", [P, 2, 1])
        minus_half, eps = sb("minus_half", [P, 1]), sb("eps", [P, 1])
        v_eps = sb("v_eps", [P, 2])
        logit, top, tau, gate = (sb(n, [P, E]) for n in ("logit", "top", "tau", "gate"))
        top_sums = sb("top_sums", [P, E, E])
        tau1 = sb("tau1", [P, 1])
        hw = sb("hw", [P, ER])
        hw_hi, hw_lo = sb("hw_hi", [P, P], F32R), sb("hw_lo", [P, P], F32R)
        w_mean = sb("w_mean", [P, NB])
        zero_row = sb("zero_row", [1, P])
        ar_raw_t = sb("ar_raw", [P, NB, AR])
        ar_raw = ar_raw_t[:, :, :]
        kpad = nc.dram_tensor("kpad", [1, P + L], F32, kind="Internal").ap()

        p_x = psum("p_x", 512)
        p_a = psum("p_a", 1024)
        p_b = psum("p_b", 1024)
        p_f = psum("p_f", NC * 512)

        names = ("ld_exp ld_a ld_r ld_const ld_ssm ld_s4 ld_s4b ld_w0 ld_w1 ld_ar ld_misc ld_x0 ld_x1 k_out k_back stored0 stored1 "
                 "v_chain g_chain p_chain v_step g_step consts_g "
                 "exp_done em1_done coeff s4_d s4_sq s4_v s4_sum s4_at s4_b s4_k s4_kt s4_ktc t_rev t_hi_s t_split cum_mm cum_done "
                 "ssm_r ssm_s a_abs planes planes_t planes_c size_e size_done lb_hi_s lb_done "
                 "w_mean w_cent w_tr w_hi_s w_lo_s r_tr r_evac ar_mean ar_cent ar_done "
                 "angles waves turn_low power_done x_sw x_t g_prod g_done g_hi_s g_split q_done q_hi_s q_split "
                 "h1T h1_t h1hi h1lo h1row h1_sb mvar1 rs1 y_mm h2_s h2T h2hi h2lo mvar2 rs2 h2b "
                 "ar_mm base0 gated hwT hw_split o_mm fin").split()
        S = {n: sem(n) for n in names}
        block = ctx.enter_context(nc.Block())

        def chain(eng, name):
            count = [0]

            def link(ins):
                count[0] += 1
                ins.then_inc(S[name], 1)
                eng.wait_ge(S[name], count[0])
            return link

        SMALL = 48
        size_flat = size[:, :, :].rearrange("p h j -> p (h j)")
        small = size_flat[:, 0:SMALL * (N + 2)].rearrange("p (n w) -> p n w", n=SMALL)
        planes = size_flat[:, SMALL * (N + 2):SMALL * (N + 2) + 7 * P].rearrange("p (f n) -> p f n", f=7)

        def sm(n, w=N):
            return small[:, n, 0:w]

        LH = L // 2
        s4_cos, s4_sin = (g[:, :, :, :].rearrange("p t a c -> p (t a c)")[:, 0:LH] for g in (g_a, g_b))
        inv_re, inv_im = h1[:, 0:LH], h2[:, 0:LH]
        s4_wr, s4_wi = small[:, 31, 0:8], small[:, 31, 8:16]
        ssm_b = q_a[:, 1, :].rearrange("p (n r) -> p n r", r=2)
        vc = q_b[:, 1, :].rearrange("p (n r) -> p n r", r=2)
        twiddle = q_a[:, 0, :]

        t_rev = h1_t[:, :, :].rearrange("p k c -> p (k c)")
        lora_b = h1[:, :]
        cls_row = h2[0:1, :]
        router_rows = h1_t[0:E, :, :].rearrange("p k c -> p (k c)")
        k_rows = hw[0:NB, :]
        x_rows = a["x"].rearrange("c h n r -> c h (n r)")

        def heads(t):
            return bass.ds(TH * (t - 1), TH)

        def flat(t):
            return t[:, :, :, :].rearrange("p h a c -> p (h a c)")

        by_head_psum = p_a[:, :].rearrange("p (h a c) -> p h a c", h=TH, a=NB)

        def by_head(t):
            return t[:, :, :].rearrange("p a (h c) -> p h a c", h=TH)

        def bcast(ap, axis, count):
            shape = list(ap.shape)
            shape.insert(axis, count)
            return ap.unsqueeze(axis).broadcast_to(shape)

        def steps(eng, step):
            for t in range(3):
                step(t, t % 2, (t - 1) // 2)
            with eng.Fori(1, TILES // 2 - 1) as i:
                step(2 * i + 1, 1, i)
                step(2 * i + 2, 0, i)
            for t in range(TILES - 1, TILES + 2):
                step(t, t % 2, (t - 1) // 2)

        def step_chain(eng, name):
            count = [0]

            def own(ins):
                count[0] += 1
                ins.then_inc(S[name], 1)

            def start():
                count[0] = 0
                eng.sem_clear(S[name])
            own.start, own.wait = start, lambda: eng.wait_ge(S[name], count[0])
            return own

        mul, add, sub = ALU.mult, ALU.add, ALU.subtract
        ex = sm(2, N + 2)
        ea, dt, s4_step = ex[:, 0:N], ex[:, N:N + 1], ex[:, N + 1:N + 2]
        turns_h, turns_l, cr, ci = sm(42), sm(43), sm(33), sm(34)
        alpha, em1, a_inv = sm(38), sm(40), sm(37)
        phase, sin_om, sin_half = sm(46), sm(47), sm(45)

        def arithmetic(eng, link, scratch=None):
            def ts(o, i, s1, s2=None, op0=ALU.mult, op1=None):
                link(eng.tensor_scalar(o, i, s1, s2, op0, op1) if op1 is not None else eng.tensor_scalar(o, i, s1, None, op0))

            def tt(o, x, y, op):
                link(eng.tensor_tensor(o, x, y, op))

            def stt(o, x, s, y, op0=ALU.mult, op1=ALU.add):
                if scratch is None:
                    link(eng.scalar_tensor_tensor(out=o, in0=x, scalar=s, in1=y, op0=op0, op1=op1))
                else:
                    ts(scratch, x, s, op0=op0)
                    tt(o, scratch, y, op1)

            def copy(o, i):
                link(eng.tensor_copy(o, i))

            def exp_parts(x, w, k, r, p, two):
                ts(k, x, 1.4426950408889634, MAGIC, mul, add)
                ts(k, k, -MAGIC, -126.0, add, ALU.max)
                stt(r, k, -LN2_PARTS[0], x)
                stt(r, k, -LN2_PARTS[1], r)
                series = exp_series()
                ts(p, r, series[0])
                for c in series[1:]:
                    stt(p, p, c, r, add, mul)
                ts(k, k, 127.0, 127.0, ALU.min, add)
                ts(two.bitcast(I32), k, float(2 ** 23))
            return ts, tt, stt, copy, exp_parts

        @block.sync
        def _(sp):
            def load(dst, src, s):
                sp.dma_start(dst, src).then_inc(S[s], 16)

            def twice(t):
                return t.rearrange("(a n) r -> a n r", a=2)

            load(small[:, 0, 0:N], a["L0_tok_inv_A_real"], "ld_exp")
            load(small[:, 0, N:N + 1], a["L0_tok_log_dt"].rearrange("(h a) -> h a", a=1), "ld_exp")
            load(small[:, 0, N + 1:N + 2], raw(a["L0_attn_log_step"], 0, [[0, P], [1, 1]]), "ld_exp")
            load(sm(1), a["L0_tok_A_imag"], "ld_a")
            load(vc, raw(a["L0_attn_Vc_ri"], 0, [[0, 2], [2 * N, N], [1, 2 * N]]), "ld_s4")
            load(sm(7), raw(a["L0_attn_Bp"], 0, [[0, P], [1, N]]), "ld_s4")
            for n, name in enumerate(("L0_attn_Lambda_ri", "L0_attn_Ct_ri", "L0_attn_p_ri", "L0_attn_q_ri")):
                load(small[:, 4, 2 * n:2 * n + 2], raw(a[name], 0, [[0, 2], [2, N], [1, 2]]), "ld_s4")
            load(s4_cos, raw(a["k_half"], 0, [[LH, 2], [0, N], [1, LH]]), "ld_s4")
            load(s4_sin, raw(a["k_half"], L, [[LH, 2], [0, N], [1, LH]]), "ld_s4")
            load(ssm_b, a["L0_tok_B"], "ld_ssm")
            load(powers[:, :], a["k_powers"], "ld_ssm")
            for i in range(2):
                load(res[:, i, :], a["L0_ffn_W_base"][i * P:(i + 1) * P, :], f"ld_w{i % 2}")
            load(ident4[:, :], a["k_ident"], "ld_const")
            load(sm(8, NB), raw(a["k_half"], 0, [[NB, P], [1, NB]]), "ld_s4b")
            load(sm(9, NB), raw(a["k_half"], L, [[NB, P], [1, NB]]), "ld_s4b")
            load(small[0:1, 10, 0:1], raw(a["L0_attn_D"], 0, [[1, 1], [1, 1]]), "ld_s4b")
            load(twiddle, a["k_twiddle"], "ld_s4b")
            load(router_rows, a["L0_ffn_W_router"], "ld_r")

            def load_w(i):
                sp.wait_ge(S["w_cent"], i - 1)
                load(res[:, i % 2, :], a["L0_ffn_W_base"][i * P:(i + 1) * P, :], f"ld_w{i % 2}")

            load_w(2)
            load_w(3)
            for k in range(NB):
                load(ar_raw[:, k, 0:ER].rearrange("p (e r) -> p e r", e=E),
                     raw(a["L0_ffn_lora_A"], k * P * RK, [[RK, P], [L * RK, E], [1, RK]]), "ld_ar")
            for t in (1, 2):
                load(x_in[:, t % 2, :, :], x_rows[:, TH * (t - 1):TH * t, :], f"ld_x{t % 2}")
            sp.wait_ge(S["s4_sum"], 1)
            load(lora_b, a["L0_ffn_lora_B"].rearrange("e r o -> (e r) o"), "ld_misc")
            load(cls_row, a["cls_tok"].rearrange("a b l -> (a b) l"), "ld_misc")
            load(bias[:, :], raw(a["L0_ffn_b_base"], 0, [[0, P], [1, L]]), "ld_misc")
            load(b_router[:, :], raw(a["L0_ffn_b_router"], 0, [[0, P], [1, E]]), "ld_misc")
            load(sparse[:, :], a["k_sparse"], "ld_misc")
            sp.wait_ge(S["p_chain"], 2)
            sp.dma_start(raw(kpad, 0, [[P, 1], [1, P]]), zero_row[:, :]).then_inc(S["k_out"], 16)
            load_w(4)
            sp.wait_ge(S["s4_ktc"], 1)
            sp.dma_start(raw(kpad, P, [[P, NB], [1, P]]), k_rows).then_inc(S["k_out"], 16)
            load_w(5)
            sp.wait_ge(S["k_out"], 32)
            sp.wait_ge(S["r_tr"], 1)
            sp.dma_start(t_rev, raw(kpad, 1, [[1, P], [1, L]])).then_inc(S["k_back"], 16)
            load_w(6)
            load_w(7)

            def load_x(t, par):
                load(x_in[:, par, :, :], x_rows[:, bass.ds(TH * (t - 1), TH), :], f"ld_x{par}")

            def store(t, par):
                for k in range(TH):
                    dst = out[:, bass.ds(TH * t + k - 1, 1), :].rearrange("c a l -> c (a l)")
                    sp.dma_start(dst, res[k * C:(k + 1) * C, par, :]).then_inc(S[f"stored{par}"], 16)

            sp.wait_ge(S["x_t"], 1)
            load_x(3, 1)
            sp.wait_ge(S["fin"], NC)
            sp.dma_start(out[:, 0:1, :].rearrange("c a l -> c (a l)"), res[0:C, 0, :]).then_inc(S["stored0"], 16)

            def turn(t, par, more):
                if more:
                    sp.wait_ge(S["x_t"], t + 1)
                    load_x(t + 3, 1 - par)
                sp.wait_ge(S["fin"], NC * t + NC)
                store(t, par)
            with sp.Fori(0, TILES // 2 - 2) as i:
                turn(2 * i + 1, 1, True)
                turn(2 * i + 2, 0, True)
            for t in range(TILES - 3, TILES + 1):
                turn(t, t % 2, t + 3 <= TILES)
            sp.wait_ge(S["stored0"], 16 + 32 * (TILES // 2))
            sp.wait_ge(S["stored1"], 32 * (TILES // 2))

        def toeplitz(pe, lhs_hi, lhs_lo, out_bank, name):
            for bank in range(2):
                lo, hi = 512 * bank, 512 * bank + 512
                blocks = range(hi // P)
                for j in blocks:
                    first = max(lo, j * P)
                    o = out_bank[:, first:hi]
                    w = slice(first - j * P, hi - j * P)
                    pe.matmul(o, lhs_hi(j), t_hi[:, w], start=(j == 0), stop=False)
                    last = pe.matmul(o, lhs_hi(j), t_lo[:, w], start=False, stop=(j == blocks[-1] and lhs_lo is None))
                    if lhs_lo is not None:
                        last = pe.matmul(o, lhs_lo(j), t_hi[:, w], start=False, stop=(j == blocks[-1]))
                last.then_inc(S[name], 1)

        def product(c):
            return slice(512 * c, 512 * c + CUTS[c + 1] - CUTS[c]), slice(CUTS[c], CUTS[c + 1])

        p_s = p_f[:, 1024:1536]
        w_turned = (p_b[:, :], p_f[:, 0:1024])

        @block.tensor
        def _(pe):
            def turn_w(i):
                pe.wait_ge(S["w_cent"], i + 1)
                if i >= 2:
                    pe.wait_ge(S["w_hi_s"], i - 1)
                    pe.wait_ge(S["w_lo_s"], i - 1)
                for k in range(NB):
                    last = pe.transpose(w_turned[i % 2][:, k * P:(k + 1) * P], h2_bias[:, i % 2, k * P:(k + 1) * P], ident)
                last.then_inc(S["w_tr"], 1)

            pe.wait_ge(S["ld_const"], 16)
            turn_w(0)
            turn_w(1)
            pe.wait_ge(S["s4_v"], 1)
            for q in range(NB):
                for half in range(2):
                    rows = slice(half * N, half * N + N)
                    o = p_s[rows, NB * q:NB * q + NB]
                    pe.matmul(o, inv_re[rows, q::NB], s4_wr[rows, :], start=True, stop=False)
                    last = pe.matmul(o, inv_im[rows, q::NB], s4_wi[rows, :], start=False, stop=True)
            last.then_inc(S["s4_sum"], 1)
            pe.wait_ge(S["ld_r"], 16)
            for k in range(NB):
                last = pe.transpose(p_x[:, E * k:E * k + E], router_rows[:, k * P:(k + 1) * P], ident[0:E, 0:E])
            last.then_inc(S["r_tr"], 1)
            pe.wait_ge(S["s4_at"], 1)
            pe.matmul(p_s[:, 64:80], dft_cos, small[:, 29, 0:16], start=True, stop=False)
            pe.matmul(p_s[:, 64:80], dft_sin, small[:, 30, 0:16], start=False, stop=True).then_inc(S["s4_b"], 1)
            pe.wait_ge(S["s4_k"], 1)
            pe.transpose(p_s[0:NB, 128:256], small[:, 28, 0:NB], ident).then_inc(S["s4_kt"], 1)
            turn_w(2)
            pe.wait_ge(S["planes"], 11)
            for f in range(7):
                last = pe.transpose(p_a[:, f * P:(f + 1) * P], planes[:, f, :], ident)
            last.then_inc(S["planes_t"], 1)
            turn_w(3)
            pe.wait_ge(S["k_back"], 16)
            pe.wait_ge(S["planes_c"], 1)
            for bank in range(2):
                last = pe.matmul(p_a[:, 512 * bank:512 * bank + 512], exch, t_rev[:, 512 * bank:512 * bank + 512],
                                 start=True, stop=True)
            last.then_inc(S["t_rev"], 1)
            turn_w(4)
            pe.wait_ge(S["r_evac"], 1)
            pe.wait_ge(S["ld_ar"], 16 * NB)
            for k in range(NB):
                last = pe.matmul(p_x[:, 128:128 + AR], ones[:, :], ar_raw[:, k, :], start=(k == 0), stop=(k == NB - 1))
            last.then_inc(S["ar_mean"], 1)
            pe.wait_ge(S["t_hi_s"], 1)
            pe.wait_ge(S["t_split"], 1)
            pe.wait_ge(S["consts_g"], 2)
            toeplitz(pe, lambda j: ones_r[:, :], None, p_a, "cum_mm")
            turn_w(5)
            turn_w(6)
            pe.wait_ge(S["cum_done"], 1)
            pe.wait_ge(S["ld_misc"], 80)
            pa = p_a[:, :].rearrange("p (h a c) -> p h a c", h=TH, a=NB)
            for h in range(TH):
                for k in range(NB):
                    last = pe.matmul(pa[:, h, k, :], cls_row[:, k * P:(k + 1) * P], ones[0:1, 0:C], start=True, stop=True)
            last.then_inc(S["h1T"], 1)
            turn_w(7)
            pe.wait_ge(S["w_lo_s"], NB)
            pe.wait_ge(S["ar_done"], 2)
            pe.wait_ge(S["lb_done"], 1)

            def three(o, x_hi, x_lo, y_hi, y_lo, start, stop):
                pe.matmul(o, x_hi, y_hi, start=start, stop=False)
                pe.matmul(o, x_hi, y_lo, start=False, stop=False)
                return pe.matmul(o, x_lo, y_hi, start=False, stop=stop)

            def step(t, par, turn):
                n = t if isinstance(t, int) else None
                cur, feed, nxt = n is None or n <= TILES, n is None or n >= 1, n is None or n < TILES
                prv = 1 - par
                if nxt:
                    pe.wait_ge(S["x_sw"], t + 1)
                    if feed:
                        pe.wait_ge(S["g_prod"], t)
                if cur:
                    pe.wait_ge(S["h1hi"], t + 1)
                    pe.wait_ge(S["h1lo"], t + 1)
                    if feed:
                        pe.wait_ge(S["h2lo"], t)
                    for k in range(NB):
                        last = pe.transpose(p_b[:, k * P:(k + 1) * P], h1_t[:, k, :], ident)
                    last.then_inc(S["h1row"], 1)
                if nxt:
                    for h in range(TH):
                        pe.transpose(p_x[:, h * C:(h + 1) * C], x_in[:, prv, h, :], ident[0:C, 0:C])
                        last = pe.transpose(p_x[:, (TH + h) * C:(TH + h + 1) * C], x_swap[:, prv, h, :], ident[0:C, 0:C])
                    last.then_inc(S["x_t"], 1)
                if cur:
                    toeplitz(pe, lambda j: h1_hi[:, j, :], lambda j: h1_lo[:, j, :], p_a, "y_mm")
                if feed:
                    feed_forward(t, prv, 0, n)
                if cur:
                    pe.wait_ge(S["h2_s"], 2 * t + 2)
                    pe.wait_ge(S["h1_sb"], t + 1)
                    for k in range(NB):
                        last = pe.transpose(p_b[:, k * P:(k + 1) * P], h2[:, k * P:(k + 1) * P], ident)
                    last.then_inc(S["h2T"], 1)
                if nxt:
                    pe.wait_ge(S["g_split"], t + 1)
                    pe.wait_ge(S["q_split"], t + 1)
                    for h in range(TH):
                        g_of = [g[:, h, :, :].rearrange("p a c -> p (a c)") for g in (g_hi, g_lo)]
                        last = three(p_a[:, h * 512:(h + 1) * 512], q_hi[:, h, :], q_lo[:, h, :], *g_of, True, True)
                    last.then_inc(S["h1T"], 1)
                if feed:
                    feed_forward(t, prv, 1, n)
                    pe.wait_ge(S["gated"], t)
                    pe.transpose(p_x[:, 256:384], hw[:, :], ident).then_inc(S["hwT"], 1)
                    feed_forward(t, prv, 2, n)
                    pe.wait_ge(S["hw_split"], 2 * t)
                    for c in range(NC):
                        bank, w = product(c)
                        at = c * 512 + (AR if c == 0 else 0)
                        o = slice(w.start - AR if c else 0, w.stop - AR)
                        if c == 0:
                            pe.wait_ge(S["base0"], t)
                        three(p_f[:, at:bank.stop], hw_hi[:, :], hw_lo[:, :], lb_hi[:, o], lb_lo[:, o], c == 0, True)\
                            .then_inc(S["o_mm"], 1)

            def feed_forward(t, prv, c, n):
                if n is None or n >= 2:
                    pe.wait_ge(S["fin"], NC * (t - 2) + c + 1)
                bank, w = product(c)
                for k in range(NB):
                    last = three(p_f[:, bank], h2_hi[:, prv, k, :], h2_lo[:, prv, k, :], wa_hi[:, k, w], wa_lo[:, k, w],
                                 k == 0, c == 0 and k == NB - 1)
                if c == 0:
                    last.then_inc(S["ar_mm"], 1)

            steps(pe, step)

        @block.scalar
        def _(act):
            def mean_w(i):
                act.wait_ge(S[f"ld_w{i % 2}"], 16 * (i // 2 + 1))
                if i >= 2:
                    act.wait_ge(S["w_tr"], i - 1)
                act.activation(h2_bias[:, i % 2, :], res[:, i % 2, :], ACT.Copy, scale=-1.0 / L,
                               accum_out=w_mean[:, i:i + 1]).then_inc(S["w_mean"], 1)

            def turned(i):
                return w_turned[i % 2].rearrange("p (k o) -> p k o", k=NB)

            def high_w(i):
                act.wait_ge(S["w_tr"], i + 1)
                act.activation(wa_hi[:, :, AR + i * P:AR + (i + 1) * P], turned(i), ACT.Copy).then_inc(S["w_hi_s"], 1)

            def waves(t):
                act.wait_ge(S["angles"], t)
                if isinstance(t, int) and t == 1:
                    pass
                else:
                    act.wait_ge(S["power_done"], t - 1)
                act.activation(wave[:, :, :, :], angle[:, :, :, :], ACT.Sin, scale=TWO_PI).then_inc(S["waves"], 1)

            mean_w(0)
            act.wait_ge(S["ssm_r"], 1)
            act.activation(sin_om, phase, ACT.Sin).then_inc(S["ssm_s"], 1)
            act.activation(sin_half, phase, ACT.Sin, scale=0.5).then_inc(S["ssm_s"], 1)
            act.wait_ge(S["s4_d"], 1)
            act.activation(s4_sin, inv_re, ACT.Square).then_inc(S["s4_sq"], 1)
            act.activation(s4_cos, inv_im, ACT.Square).then_inc(S["s4_sq"], 1)
            mean_w(1)
            act.wait_ge(S["ld_const"], 16)
            act.activation(ident_r[:, :], ident, ACT.Copy).then_inc(S["consts_g"], 1)
            act.wait_ge(S["p_chain"], 2)
            act.activation(ones_r[:, :], ones[:, :], ACT.Copy).then_inc(S["consts_g"], 1)
            for i in range(2):
                high_w(i)
                mean_w(i + 2)
            act.wait_ge(S["coeff"], 1)
            pv = planes.rearrange("p f (n r) -> p f n r", r=2)
            for f, t in ((0, alpha), (1, turns_h), (2, turns_l)):
                act.activation(pv[:, f], bcast(t, 2, 2), ACT.Copy).then_inc(S["planes"], 1)
            for f, even, odd in ((3, (cr, 1.0), (ci, 1.0)), (4, (ci, 1.0), (cr, -1.0)),
                                 (5, (ci, -1.0), (cr, -1.0)), (6, (cr, 1.0), (ci, -1.0))):
                for half, (t, sign) in enumerate((even, odd)):
                    act.activation(pv[:, f, :, half], t, ACT.Copy, scale=sign).then_inc(S["planes"], 1)
            for i in (2, 3):
                high_w(i)
                mean_w(i + 2)
            act.wait_ge(S["t_rev"], 1)
            act.activation(t_hi[:, :], p_a[:, :], ACT.Copy).then_inc(S["t_hi_s"], 1)
            high_w(4)
            mean_w(6)
            act.wait_ge(S["size_e"], 1)
            act.activation(size_flat, size_flat, ACT.Exp).then_inc(S["size_done"], 1)
            act.wait_ge(S["cum_mm"], 2)
            act.activation(neg_cum[:, :], p_a[:, :], ACT.Copy, scale=-1.0).then_inc(S["cum_done"], 1)
            high_w(5)
            mean_w(7)
            waves(1)
            act.wait_ge(S["ar_cent"], 1)
            act.activation(wa_hi[:, :, 0:AR], ar_raw, ACT.Copy).then_inc(S["ar_done"], 1)
            act.wait_ge(S["ld_misc"], 80)
            act.activation(lb_hi[:, :], lora_b, ACT.Copy).then_inc(S["lb_hi_s"], 1)
            high_w(6)

            def high_q(t):
                act.wait_ge(S["q_done"], t)
                act.activation(q_hi[:, :, :], q_a[:, :, :], ACT.Copy).then_inc(S["q_hi_s"], 1)

            def high_g(t):
                act.wait_ge(S["g_done"], t)
                act.activation(flat(g_hi), flat(g_a), ACT.Copy).then_inc(S["g_hi_s"], 1)

            def take_h1(t):
                act.wait_ge(S["h1T"], t + 1)
                act.activation(by_head(h1_t), by_head_psum, ACT.Copy).then_inc(S["h1_t"], 1)
                act.wait_ge(S["h1_t"], t + 1)
                act.activation(h1_hi[:, :, :], h1_t[:, :, :], ACT.Copy).then_inc(S["h1hi"], 1)

            take_h1(0)
            high_w(7)
            high_q(1)

            def step(t, par, turn):
                n = t if isinstance(t, int) else None
                cur, feed, nxt = n is None or n <= TILES, n is None or n >= 1, n is None or n < TILES
                if cur:
                    act.wait_ge(S["h1row"], t + 1)
                    if feed:
                        act.wait_ge(S["h2_s"], 2 * t)
                    act.activation(h1[:, :], p_b[:, :], ACT.Copy).then_inc(S["h1_sb"], 1)
                if nxt:
                    high_g(t + 1)
                if cur:
                    act.wait_ge(S["h2T"], t + 1)
                    act.activation(h2_hi[:, par, :, :].rearrange("p k c -> p (k c)"), p_b[:, :], ACT.Copy).then_inc(S["h2hi"], 1)
                if nxt:
                    take_h1(t + 1)
                if feed:
                    act.wait_ge(S["hwT"], t)
                    if n is None or n >= 2:
                        act.wait_ge(S["o_mm"], NC * (t - 1))
                    act.activation(hw_hi[:, :], p_x[:, 256:384], ACT.Copy).then_inc(S["hw_split"], 1)
                if n is None or n < TILES - 1:
                    waves(t + 2)
                    high_q(t + 2)

            steps(act, step)

        @block.gpsimd
        def _(pool):
            pool.memset(ones[:, :], 1.0).then_inc(S["p_chain"], 1)
            pool.memset(zero_row[:, :], 0.0).then_inc(S["p_chain"], 1)
            pool.memset(minus_half[:, :], -0.5).then_inc(S["p_chain"], 1)
            pool.memset(eps[:, :], EPS).then_inc(S["p_chain"], 1)
            ts, tt, stt, copy, exp_parts = arithmetic(pool, chain(pool, "g_chain"), sm(12))

            def centre_w(i):
                pool.wait_ge(S["w_mean"], i + 1)
                pool.tensor_scalar(h2_bias[:, i % 2, :], res[:, i % 2, :], w_mean[:, i:i + 1], 1.0, ALU.add, ALU.mult)\
                    .then_inc(S["w_cent"], 1)

            pool.wait_ge(S["exp_done"], 1)
            pool.wait_ge(S["ld_a"], 16)
            a_im, om, k = sm(1), sm(39), sm(33)
            ts(om, a_im, dt)
            ts(k, om, INV_2PI, MAGIC, mul, add)
            ts(k, k, -MAGIC, None, add)
            stt(phase, k, -PI_PARTS[0], om)
            stt(phase, k, -PI_PARTS[1], phase)
            stt(phase, k, -PI_PARTS[2], phase)
            pool.tensor_scalar(phase, phase, 3.1415925, -3.1415925, ALU.min, ALU.max).then_inc(S["ssm_r"], 1)
            pool.wait_ge(S["ssm_r"], 1)
            turns = sm(41)
            ts(turns, phase, INV_2PI)
            ts(turns_h, turns, MAGIC13, -MAGIC13, add, add)
            tt(turns_l, turns, turns_h, sub)
            centre_w(0)
            centre_w(1)
            pool.wait_ge(S["ssm_s"], 2)
            s1, s2 = sin_om, sin_half
            er, ei = sm(33), sm(34)
            tt(s2, s2, s2, mul)
            ts(er, s2, -2.0, 1.0, mul, add)
            pool.wait_ge(S["em1_done"], 1)
            tt(er, er, em1, mul)
            stt(er, s2, -2.0, er)
            stt(ei, em1, 1.0, s1, add, mul)
            tmp, nr, ni = sm(36), sm(44), sm(32)
            tt(nr, ei, a_im, mul)
            tt(tmp, er, ea, mul)
            tt(nr, nr, tmp, sub)
            tt(ni, er, a_im, mul)
            tt(tmp, ei, ea, mul)
            tt(ni, ni, tmp, add)
            pool.wait_ge(S["a_abs"], 1)
            tt(nr, nr, a_inv, mul)
            tt(ni, ni, a_inv, mul)
            pool.wait_ge(S["ld_ssm"], 32)
            br, bi = ssm_b[:, :, 0], ssm_b[:, :, 1]
            tt(cr, nr, br, mul)
            tt(tmp, ni, bi, mul)
            tt(cr, cr, tmp, add)
            tt(ci, nr, bi, mul)
            tt(tmp, ni, br, mul)
            tt(ci, ci, tmp, sub)
            pool.sem_inc(S["coeff"], 1)
            for i in range(2, 6):
                centre_w(i)

            def swap(par):
                for r in range(2):
                    ins = pool.tensor_copy(x_swap[:, par, :, r::2], x_in[:, par, :, 1 - r::2])
                ins.then_inc(S["x_sw"], 1)

            own = step_chain(pool, "g_step")

            def turns_low(t):
                pool.tensor_tensor(turn_l[:, :, :], bcast(planes_t[:, 2, heads(t)], 2, PW), bcast(powers[:, 0:PW], 1, TH), ALU.mult)\
                    .then_inc(S["turn_low"], 1)

            def make_powers(t, par):
                pool.wait_ge(S["waves"], t)
                own(pool.tensor_tensor(power[:, par, :, :, :], wave[:, :, :, :], bcast(size[:, heads(t), :], 1, 2), ALU.mult))
                own.wait()
                for k in range(2):
                    f = 3 + 2 * k
                    own(pool.tensor_tensor(uw_prod[:, k, :, :, :], power[:, par, :, :, 0:NB],
                                           bcast(planes_t[:, f:f + 2, heads(t)], 3, NB), ALU.mult))
                own.wait()
                last = pool.tensor_tensor(uw[:, par, :, :, :], uw_prod[:, :, 0, :, :], uw_prod[:, :, 1, :, :], ALU.add)
                last.then_inc(S["power_done"], 1)

            def make_q(par):
                z16 = [power[:, par, k, :, NB:NB + NE] for k in range(2)]
                z1_sin, z1_cos = (power[:, par, k, :, NB + NE:PW] for k in range(2))
                for q, x, y in ((q_a, z16[0], z1_cos), (q_b, z16[1], z1_sin)):
                    own(pool.tensor_tensor(q[:, :, :].rearrange("p h (i j) -> p h i j", i=NE), bcast(x, 3, NF), bcast(y, 2, NE), ALU.mult))
                own.wait()
                pool.tensor_tensor(q_a[:, :, :], q_a[:, :, :], q_b[:, :, :], ALU.add).then_inc(S["q_done"], 1)

            def step(t, par, turn):
                n = t if isinstance(t, int) else None
                cur, feed, nxt = n is None or n <= TILES, n is None or n >= 1, n is None or n < TILES
                prv = 1 - par
                own.start()
                if nxt:
                    pool.wait_ge(S["q_hi_s"], t + 1)
                    pool.wait_ge(S["h1T"], t + 1)
                    if n is None or n < TILES - 1:
                        pool.wait_ge(S["angles"], t + 1)
                    pool.tensor_tensor(q_lo[:, :, :], q_a[:, :, :], q_hi[:, :, :].bitcast(F32), ALU.subtract).then_inc(S["q_split"], 1)
                if n is None or n < TILES - 1:
                    turns_low(t + 2)
                if nxt:
                    pool.wait_ge(S["g_prod"], t + 1)
                    pool.tensor_tensor(flat(g_a), flat(g_a), flat(g_b), ALU.add).then_inc(S["g_done"], 1)
                if cur:
                    pool.wait_ge(S["mvar1"], t + 1)
                    if feed:
                        pool.wait_ge(S["h2_s"], 2 * t)
                    own(pool.tensor_tensor(v_eps[:, 0:1], mv1[:, 1:2], eps[:, :], ALU.add))
                    own.wait()
                    pool.tensor_tensor(rstd1[:, :], v_eps[:, 0:1], minus_half[:, :], ALU.pow).then_inc(S["rs1"], 1)
                if nxt:
                    pool.wait_ge(S["g_hi_s"], t + 1)
                    if n is None or n < TILES - 1:
                        if n is None or n >= 1:
                            pool.wait_ge(S["x_t"], t)
                        pool.wait_ge(S[f"ld_x{par}"], 16 * (turn + 2))
                    pool.tensor_tensor(flat(g_lo), flat(g_a), flat(g_hi).bitcast(F32), ALU.subtract).then_inc(S["g_split"], 1)
                if n is None or n < TILES - 1:
                    swap(par)
                if cur:
                    pool.wait_ge(S["h2_s"], 2 * t + 2)
                    if n is None or n >= 2:
                        pool.wait_ge(S["fin"], NC * (t - 1))
                    pool.tensor_tensor(h2_bias[:, par, :], h2[:, :], bias[:, :], ALU.add).then_inc(S["h2b"], 1)
                    pool.wait_ge(S["mvar2"], t + 1)
                    own(pool.tensor_tensor(v_eps[:, 1:2], mv2[:, 1:2], eps[:, :], ALU.add))
                    own.wait()
                    pool.tensor_tensor(rstd2[:, par, :], v_eps[:, 1:2], minus_half[:, :], ALU.pow).then_inc(S["rs2"], 1)
                if n is None or n < TILES - 1:
                    make_powers(t + 2, par)
                    make_q(par)

            own.start()
            pool.wait_ge(S["planes_c"], 1)
            pool.wait_ge(S["ld_x1"], 16)
            turns_low(1)
            for i in range(6, NB):
                centre_w(i)
            pool.wait_ge(S["ar_done"], 1)
            pool.tensor_tensor(wa_lo[:, :, 0:AR], ar_raw, wa_hi[:, :, 0:AR].bitcast(F32), ALU.subtract).then_inc(S["ar_done"], 1)
            pool.wait_ge(S["lb_hi_s"], 1)
            pool.tensor_tensor(lb_lo[:, :], lora_b, lb_hi[:, :].bitcast(F32), ALU.subtract).then_inc(S["lb_done"], 1)
            swap(1)
            pool.wait_ge(S["size_done"], 1)
            make_powers(1, 1)
            make_q(1)
            steps(pool, step)

        @block.vector
        def _(dve):
            link = chain(dve, "v_chain")

            ts, tt, stt, copy, exp_parts = arithmetic(dve, link)

            dve.wait_ge(S["ld_exp"], 48)
            w = N + 2
            x0, k, r, p, two = (sm(n, w) for n in (0, 13, 14, 15, 16))
            exp_parts(x0, w, k, r, p, two)
            stt(ex, p, 1.0, two, add, mul)
            dve.sem_inc(S["exp_done"], 1)
            dve.wait_ge(S["ld_a"], 16)
            tmp = sm(11)
            tt(a_inv, sm(1), sm(1), mul)
            tt(tmp, ea, ea, mul)
            tt(a_inv, a_inv, tmp, add)
            ts(a_inv, a_inv, 0.5)
            dve.reciprocal(a_inv, a_inv).then_inc(S["a_abs"], 1)

            dve.wait_ge(S["ld_s4"], 16 * 8)
            lam = small[:, 4, 0:2]
            sv = small[:, 16, 0:4].rearrange("p (v r) -> p v r", v=2)
            prod = small[:, 17:19, 0:N]
            tt(prod, vc.rearrange("p n r -> p r n"), bcast(sm(7), 1, 2), mul)
            link(dve.tensor_reduce(sv[:, 0, :], prod, AX.X, add))
            copy(sv[:, 1, :], small[:, 4, 4:6])
            vv = small[:, 17, 0:8].rearrange("p (m v r) -> p m v r", m=2, v=2)
            t2 = small[:, 18, 0:2]
            for m, at in enumerate((2, 6)):
                mr, mi = small[:, 4, at:at + 1], small[:, 4, at + 1:at + 2]
                ts(t2, sv[:, :, 0], mr)
                stt(vv[:, m, :, 0], sv[:, :, 1], mi, t2)
                ts(t2, sv[:, :, 0], mi)
                stt(vv[:, m, :, 1], sv[:, :, 1], mr, t2, mul, sub)
            vj = small[:, 17, 0:8].rearrange("p (j r) -> p j r", r=2)
            wr, wi = (x.rearrange("p (j r) -> p j r", r=2) for x in (s4_wr, s4_wi))
            copy(wr, vj)
            ts(wi[:, :, 0], vj[:, :, 1], -1.0)
            copy(wi[:, :, 1], vj[:, :, 0])
            g2, nl = small[:, 19, 0:1], small[:, 19, 2:4]
            link(dve.reciprocal(g2, s4_step))
            ts(g2, g2, 2.0)
            ts(nl, lam, -1.0)
            ts(inv_re, s4_cos, nl[:, 0:1])
            ts(inv_im, s4_sin, g2)
            dve.scalar_tensor_tensor(out=inv_im, in0=s4_cos, scalar=nl[:, 1:2], in1=inv_im, op0=mul, op1=add)\
                .then_inc(S["s4_d"], 1)
            dve.wait_ge(S["s4_sq"], 2)
            tt(s4_sin, s4_sin, s4_cos, add)
            link(dve.reciprocal(s4_cos, s4_sin))
            tt(inv_re, inv_re, s4_cos, mul)
            stt(inv_im, inv_im, -1.0, s4_cos, mul, mul)
            dve.sem_inc(S["s4_v"], 1)

            def low_w(i):
                dve.wait_ge(S["w_hi_s"], i + 1)
                cols = slice(AR + i * P, AR + (i + 1) * P)
                dve.tensor_tensor(wa_lo[:, :, cols], w_turned[i % 2].rearrange("p (k o) -> p k o", k=NB),
                                  wa_hi[:, :, cols].bitcast(F32), sub).then_inc(S["w_lo_s"], 1)

            low_w(0)
            k, r, p, two = (sm(n) for n in (13, 14, 15, 16))
            ts(alpha, ea, dt, -1.0, mul, mul)
            exp_parts(alpha, N, k, r, p, two)
            tt(p, two, p, mul)
            stt(em1, two, -1.0, p, add, add)
            dve.sem_inc(S["em1_done"], 1)
            dve.wait_ge(S["s4_sum"], 1)
            dve.wait_ge(S["ld_s4b"], 64)
            sums = small[:, 16, 0:N]
            copy(sums, p_s[:, 0:N])
            s = sums.rearrange("p (q j) -> p j q", q=NB)
            c8, s8 = sm(8, NB), sm(9, NB)
            tr, ti, den, tmp, xr, xi, yr, yi = (sm(n, NB) for n in (17, 18, 19, 20, 21, 22, 23, 24))
            tt(tr, c8, s[:, 6], mul)
            ts(tr, tr, 1.0, None, add)
            tt(ti, c8, s[:, 7], mul)
            tt(den, tr, tr, mul)
            tt(tmp, ti, ti, mul)
            tt(den, den, tmp, add)
            link(dve.reciprocal(den, den))
            tt(xr, s[:, 2], s[:, 4], mul)
            tt(tmp, s[:, 3], s[:, 5], mul)
            tt(xr, xr, tmp, sub)
            tt(xr, xr, c8, mul)
            tt(xi, s[:, 2], s[:, 5], mul)
            tt(tmp, s[:, 3], s[:, 4], mul)
            tt(xi, xi, tmp, add)
            tt(xi, xi, c8, mul)
            tt(yr, xr, tr, mul)
            tt(tmp, xi, ti, mul)
            tt(yr, yr, tmp, add)
            tt(yr, yr, den, mul)
            tt(yi, xi, tr, mul)
            tt(tmp, xr, ti, mul)
            tt(yi, yi, tmp, sub)
            tt(yi, yi, den, mul)
            tt(yr, s[:, 0], yr, sub)
            tt(yi, s[:, 1], yi, sub)
            at1, at2 = small[:, 29, 0:2 * NB], small[:, 30, 0:2 * NB]
            tt(xr, c8, yr, mul)
            tt(tmp, s8, yi, mul)
            tt(at1[:, 0:NB], xr, tmp, sub)
            tt(xr, c8, yi, mul)
            tt(tmp, s8, yr, mul)
            tt(at1[:, NB:], xr, tmp, add)
            ts(at2[:, 0:NB], at1[:, NB:], -1.0)
            copy(at2[:, NB:], at1[:, 0:NB])
            dve.sem_inc(S["s4_at"], 1)
            dve.wait_ge(S["s4_b"], 1)
            kp = small[:, 18:20, 0:N].rearrange("p a b -> p a b")
            spec = sm(17, 2 * NB)
            copy(spec, p_s[:, 64:80])
            tw = twiddle.rearrange("p (r q) -> p r q", r=NB)
            tt(tw, tw, bcast(spec, 1, NB), mul)
            kern = sm(28, NB)
            link(dve.tensor_reduce(kern, tw, AX.X, add))
            tt(kern[0:1, 0:1], kern[0:1, 0:1], small[0:1, 10, 0:1], add)
            dve.sem_inc(S["s4_k"], 1)
            dve.wait_ge(S["s4_kt"], 1)
            dve.tensor_copy(k_rows, p_s[0:NB, 128:256]).then_inc(S["s4_ktc"], 1)
            low_w(1)
            dve.wait_ge(S["r_tr"], 1)
            dve.tensor_copy(ar_raw[:, :, ER:AR], p_x[:, 0:NB * E].rearrange("p (k e) -> p k e", k=NB)).then_inc(S["r_evac"], 1)
            dve.wait_ge(S["planes_t"], 1)
            dve.tensor_copy(planes_t[:, :, :].rearrange("p f h -> p (f h)"), p_a[:, 0:7 * P]).then_inc(S["planes_c"], 1)
            low_w(2)
            dve.wait_ge(S["planes_c"], 1)
            dve.wait_ge(S["s4_ktc"], 1)
            dve.wait_ge(S["ld_ssm"], 32)
            dve.tensor_tensor(size[:, :, :], bcast(planes_t[:, 0, :], 2, PW), bcast(powers[:, 0:PW], 1, H), mul).then_inc(S["size_e"], 1)
            dve.wait_ge(S["t_hi_s"], 1)
            dve.tensor_tensor(t_lo[:, :], p_a[:, :], t_hi[:, :].bitcast(F32), sub).then_inc(S["t_split"], 1)
            low_w(3)
            low_w(4)
            dve.wait_ge(S["ar_mean"], 1)
            dve.scalar_tensor_tensor(out=ar_raw, in0=bcast(p_x[:, 128:128 + AR], 1, NB), scalar=-1.0 / L, in1=ar_raw,
                                     op0=mul, op1=add).then_inc(S["ar_cent"], 1)
            low_w(5)

            own = step_chain(dve, "v_step")

            def then(ins):
                own(ins)
                own.wait()

            def phases(t):
                hs = heads(t)
                then(dve.tensor_tensor(turn_f[:, :, :], bcast(planes_t[:, 1, hs], 2, PW), bcast(powers[:, 0:PW], 1, TH), mul))
                then(dve.tensor_tensor(turn_f[:, :, :], turn_f[:, :, :], bcast(powers[:, PW:2 * PW], 1, TH), add))
                dve.wait_ge(S["turn_low"], t)
                then(dve.tensor_tensor(turn_k[:, :, :], turn_f[:, :, :], turn_l[:, :, :], add))
                then(dve.tensor_scalar(turn_k[:, :, :], turn_k[:, :, :], MAGIC, -MAGIC, add, add))
                then(dve.tensor_tensor(turn_f[:, :, :], turn_f[:, :, :], turn_k[:, :, :], sub))
                if not (isinstance(t, int) and t == 1):
                    dve.wait_ge(S["waves"], t - 1)
                then(dve.tensor_tensor(angle[:, 0, :, :], turn_f[:, :, :], turn_l[:, :, :], add))
                then(dve.tensor_scalar(turn_k[:, :, :], angle[:, 0, :, :], 0.25, None, ALU.is_gt))
                dve.scalar_tensor_tensor(out=angle[:, 1, :, :], in0=angle[:, 0, :, :], scalar=0.25, in1=turn_k[:, :, :],
                                         op0=add, op1=sub).then_inc(S["angles"], 1)

            def stats(src, s):
                for half in range(2):
                    ins = dve.bn_stats(st[:, s, half, :], src[:, 512 * half:512 * half + 512])
                own(ins)

            def aggregate(s, mv, name):
                own.wait()
                dve.bn_aggr(mv[:, :], st[:, s, :, :].rearrange("p a b -> p (a b)")).then_inc(S[name], 1)

            def products(t, par):
                dve.wait_ge(S["x_t"], t)
                dve.wait_ge(S["power_done"], t)
                for k, g in enumerate((g_a, g_b)):
                    x = p_x[:, k * TH * C:(k + 1) * TH * C].rearrange("p (h c) -> p h c", h=TH)
                    ins = dve.tensor_tensor(g[:, :, :, :], bcast(x, 2, NB), bcast(uw[:, par, k, :, :], 3, C), mul)
                ins.then_inc(S["g_prod"], 1)

            def gate_step(prv):
                then(dve.scalar_tensor_tensor(out=logit[:, :], in0=p_f[:, ER:AR], scalar=rstd2[:, prv, :], in1=b_router[:, :],
                                              op0=mul, op1=add))
                then(dve.max(top[:, :], logit[:, :]))
                then(dve.tensor_tensor(top_sums[:, :, :], sparse[:, 0:E * E].rearrange("p (k i) -> p k i", k=E),
                                       bcast(top[:, :], 1, E), mul))
                then(dve.tensor_reduce(tau[:, :], top_sums[:, :, :], AX.X, add))
                then(dve.tensor_tensor(tau[:, :], tau[:, :], sparse[:, E * E:E * E + E], add))
                then(dve.tensor_reduce(tau1[:, :], tau[:, :], AX.X, ALU.max))
                then(dve.tensor_scalar(gate[:, :], logit[:, :], tau1[:, :], 0.0, sub, ALU.max))
                dve.tensor_tensor(hw[:, :].rearrange("p (e r) -> p e r", e=E), p_f[:, 0:ER].rearrange("p (e r) -> p e r", e=E),
                                  bcast(gate[:, :], 2, RK), mul).then_inc(S["gated"], 1)

            def finish(prv, c, gated=True):
                at = 512 * c + (AR if c == 0 else 0)
                cols = slice(max(CUTS[c] - AR, 0), CUTS[c + 1] - AR)
                plus = res if c == 0 and gated else h2_bias
                return dve.scalar_tensor_tensor(out=res[:, prv, cols], in0=p_f[:, at:512 * c + CUTS[c + 1] - CUTS[c]],
                                                scalar=rstd2[:, prv, :], in1=plus[:, prv, cols], op0=mul, op1=add)

            def low_h1(t):
                dve.wait_ge(S["h1hi"], t + 1)
                dve.tensor_tensor(h1_lo[:, :, :], h1_t[:, :, :], h1_hi[:, :, :].bitcast(F32), sub).then_inc(S["h1lo"], 1)

            def step(t, par, turn):
                n = t if isinstance(t, int) else None
                cur, feed, nxt = n is None or n <= TILES, n is None or n >= 1, n is None or n < TILES
                prv = 1 - par
                own.start()
                if nxt:
                    if feed:
                        dve.wait_ge(S["g_split"], t)
                    products(t + 1, prv)
                if cur:
                    dve.wait_ge(S["h1_sb"], t + 1)
                    stats(h1, 0)
                    aggregate(0, mv1, "mvar1")
                if cur and feed:
                    dve.wait_ge(S["h2T"], t)
                    dve.wait_ge(S["h2b"], t)
                    dve.wait_ge(S["rs2"], t)

                def centre(half):
                    cols = slice(512 * half, 512 * half + 512)
                    dve.wait_ge(S["y_mm"], 2 * t + 1 + half)
                    own(dve.scalar_tensor_tensor(out=h2[:, cols], in0=neg_cum[:, cols], scalar=mv1[:, 0:1], in1=p_a[:, cols],
                                                 op0=mul, op1=add))
                if cur:
                    dve.wait_ge(S["mvar1"], t + 1)
                    centre(0)
                if n is None or n < TILES - 1:
                    phases(t + 2)
                if cur:
                    centre(1)
                    dve.wait_ge(S["rs1"], t + 1)
                    for half in range(2):
                        cols = slice(512 * half, 512 * half + 512)
                        if half == 0:
                            own.wait()
                        dve.scalar_tensor_tensor(out=h2[:, cols], in0=h2[:, cols], scalar=rstd1[:, :], in1=h1[:, cols],
                                                 op0=mul, op1=add).then_inc(S["h2_s"], 1)
                    dve.wait_ge(S["h2_s"], 2 * t + 2)
                    stats(h2, 1)
                    aggregate(1, mv2, "mvar2")
                if feed:
                    dve.wait_ge(S["ar_mm"], t)
                    if not cur:
                        dve.wait_ge(S["rs2"], t)
                    gate_step(prv)
                    if n is None or n >= 3:
                        dve.wait_ge(S[f"stored{prv}"], 32 * turn - 16 * par)
                    finish(prv, 0, False).then_inc(S["base0"], 1)
                if cur:
                    dve.wait_ge(S["h2hi"], t + 1)
                    dve.tensor_tensor(h2_lo[:, par, :, :].rearrange("p k c -> p (k c)"), p_b[:, :],
                                      h2_hi[:, par, :, :].rearrange("p k c -> p (k c)").bitcast(F32), sub).then_inc(S["h2lo"], 1)
                if nxt:
                    low_h1(t + 1)
                if feed:
                    dve.wait_ge(S["hw_split"], 2 * t - 1)
                    dve.tensor_tensor(hw_lo[:, :], p_x[:, 256:384], hw_hi[:, :].bitcast(F32), sub).then_inc(S["hw_split"], 1)
                    for c in range(NC):
                        dve.wait_ge(S["o_mm"], NC * (t - 1) + 1 + c)
                        finish(prv, c).then_inc(S["fin"], 1)

            own.start()
            phases(1)
            low_w(6)
            low_w(7)
            low_h1(0)
            steps(dve, step)


_INS = ["x", "cls_tok", "L0_tok_log_dt", "L0_tok_B", "L0_tok_inv_A_real", "L0_tok_A_imag", "L0_attn_Lambda_ri",
        "L0_attn_p_ri", "L0_attn_q_ri", "L0_attn_Vc_ri", "L0_attn_Ct_ri", "L0_attn_Bp", "L0_attn_D",
        "L0_attn_log_step", "L0_ffn_W_base", "L0_ffn_b_base", "L0_ffn_W_router", "L0_ffn_b_router",
        "L0_ffn_lora_A", "L0_ffn_lora_B"]


def kernel(**inputs):
    import concourse.bacc as _bacc
    from concourse.bass_utils import run_bass_kernel_spmd as _run

    nc = _bacc.Bacc("TRN2", target_bir_lowering=False, num_devices=1)
    arrays = {name: np.ascontiguousarray(inputs[name]) for name in _INS}
    arrays.update(shape_tables())
    aps = {name: nc.dram_tensor(f"in_{name}", x.shape, mybir.dt.from_np(x.dtype), kind="ExternalInput").ap()
           for name, x in arrays.items()}
    out = nc.dram_tensor("out_0", (C, H + 1, L), F32, kind="ExternalOutput").ap()
    build(nc, aps, out)
    r = _run(nc, [{f"in_{name}": x for name, x in arrays.items()}], core_ids=[0])
    return r.results[0]["out_0"]
```
